# Optimizing a Trainium2 kernel written in Bass

```python
import numpy as np
import jax
import jax.numpy as jnp

def _softmax(x, axis=-1):
    return jax.nn.softmax(x, axis=axis)

def _gelu(x):
    return jax.nn.gelu(x, approximate=True)

def _silu(x):
    return jax.nn.silu(x)

def _sigmoid(x):
    return jax.nn.sigmoid(x)

def _layernorm(x, axis=-1, eps=1e-05):
    m = jnp.mean(x, axis=axis, keepdims=True)
    v = jnp.var(x, axis=axis, keepdims=True)
    return (x - m) / jnp.sqrt(v + eps)

def _scatter_add(tgt, idx, src, axis=0):
    return tgt.at[idx].add(src)

def _segment_sum(src, seg, n):
    return jax.ops.segment_sum(src, seg, n)
kernel_name = 'mk_early_fusion_d1_tok_img1024_r4_a0cbe5'

def setup_inputs(seed: int=0):
    np.random.seed(seed)
    _w = jnp.asarray

    def _rec_inputs():
        import jax
        import jax.numpy as jnp
        _rk = jax.random.key(seed)
        x = -0.000125008 + 0.999885 * jax.random.normal(jax.random.fold_in(_rk, 1), (4, 512, 256, 4), jnp.float32)
        txt = -8.03667e-05 + 0.656214 * jax.random.normal(jax.random.fold_in(_rk, 2), (4, 32, 256), jnp.float32)
        return (x, txt)
    x, txt = _rec_inputs()

    def _L0_tok_setup():
        import jax, jax.numpy as jnp
        import numpy as np
        key = jax.random.key(seed)
        k1, k2, k3 = jax.random.split(key, 3)
        B, H, I, O, Dp1 = (4, 512, 256, 256, 4)
        x = jax.random.normal(k1, (B, H, I, Dp1), dtype=jnp.float32)
        weight = 0.1 * jax.random.normal(k2, (O, Dp1), dtype=jnp.float32)
        weighted_sum = 0.1 * jax.random.normal(k3, (O, I), dtype=jnp.float32)
        return {'x': x, 'weight': weight, 'weighted_sum': weighted_sum}
    _L0_tok_all = _L0_tok_setup()
    _L0_tok_in = {k: v for k, v in _L0_tok_all.items() if k in ('weight', 'weighted_sum')}
    del _L0_tok_all

    def _L0_attn_setup():
        import jax, jax.numpy as jnp
        import numpy as np
        B, L, HID = (2, 512, 256)
        H = 16
        D = HID // H
        LR = 16
        EPS = 1e-05
        GLN = 16.0
        SCALE = D ** (-0.5)

        def _reference_tuple_inner(x, Wq, Wk, Wv, Wg1, Wg2, bg2, Wg, g_norm_w, Wo):
            Bb, Ll, Hid = x.shape
            q = (x @ Wq).reshape(Bb, Ll, H, D)
            k = (x @ Wk).reshape(Bb, Ll, H, D)
            v = (x @ Wv).reshape(Bb, Ll, H, D)
            gk = jax.nn.log_sigmoid(x @ Wg1 @ Wg2 + bg2).reshape(Bb, Ll, H, D) / GLN

            def step(S, inp):
                q_t, k_t, v_t, gk_t = inp
                S = jnp.exp(gk_t)[..., None] * S + k_t[..., None] * v_t[..., None, :]
                o_t = jnp.einsum('bhdv,bhd->bhv', S, q_t) * SCALE
                return (S, o_t)
            S0 = jnp.zeros((Bb, H, D, D), x.dtype)
            scan_in = tuple((jnp.moveaxis(t, 1, 0) for t in (q, k, v, gk)))
            S, o = jax.lax.scan(step, S0, scan_in)
            o = jnp.moveaxis(o, 0, 1)
            o = o * jax.lax.rsqrt(jnp.mean(o * o, axis=-1, keepdims=True) + EPS) * g_norm_w
            o = o.reshape(Bb, Ll, Hid)
            g = x @ Wg
            o = o * (g * jax.nn.sigmoid(g))
            o = o @ Wo
            return (o, S[:, None])
        key = jax.random.key(seed)
        ks = jax.random.split(key, 9)
        s = 0.02
        return {'x': jax.random.normal(ks[0], (B, L, HID), jnp.float32), 'Wq': jax.random.normal(ks[1], (HID, HID), jnp.float32) * s, 'Wk': jax.random.normal(ks[2], (HID, HID), jnp.float32) * s, 'Wv': jax.random.normal(ks[3], (HID, HID), jnp.float32) * s, 'Wg1': jax.random.normal(ks[4], (HID, LR), jnp.float32) * s, 'Wg2': jax.random.normal(ks[5], (LR, HID), jnp.float32) * s, 'bg2': jnp.zeros((HID,), jnp.float32), 'Wg': jax.random.normal(ks[6], (HID, HID), jnp.float32) * s, 'g_norm_w': jnp.ones((D,), jnp.float32), 'Wo': jax.random.normal(ks[7], (HID, HID), jnp.float32) * s}
    _L0_attn_all = _L0_attn_setup()
    _L0_attn_in = {k: v for k, v in _L0_attn_all.items() if k in ('Wq', 'Wk', 'Wv', 'Wg1', 'Wg2', 'bg2', 'Wg', 'g_norm_w', 'Wo')}
    del _L0_attn_all

    def _L0_ffn_setup():
        import math
        import jax, jax.numpy as jnp
        import numpy as np
        TOP_K = 2
        CAP_FACTOR = 1.25
        CLAMP = 10000.0
        key = jax.random.key(seed)
        k1, k2, k3, k4, k5 = jax.random.split(key, 5)
        B, S, D, F, E = (4, 512, 256, 1024, 8)
        std = 0.02
        return {'x': jax.random.normal(k1, (B, S, D), dtype=jnp.float32), 'Wr': jax.random.normal(k2, (D, E), dtype=jnp.float32) * std, 'W1': jax.random.normal(k3, (E, D, F), dtype=jnp.float32) * std, 'W3': jax.random.normal(k4, (E, D, F), dtype=jnp.float32) * std, 'W2': jax.random.normal(k5, (E, F, D), dtype=jnp.float32) * std}
    _L0_ffn_all = _L0_ffn_setup()
    _L0_ffn_in = {k: v for k, v in _L0_ffn_all.items() if k in ('Wr', 'W1', 'W3', 'W2')}
    del _L0_ffn_all
    return {'x': x, 'txt': txt, 'L0_tok_weight': _L0_tok_in['weight'], 'L0_tok_weighted_sum': _L0_tok_in['weighted_sum'], 'L0_attn_Wq': _L0_attn_in['Wq'], 'L0_attn_Wk': _L0_attn_in['Wk'], 'L0_attn_Wv': _L0_attn_in['Wv'], 'L0_attn_Wg1': _L0_attn_in['Wg1'], 'L0_attn_Wg2': _L0_attn_in['Wg2'], 'L0_attn_bg2': _L0_attn_in['bg2'], 'L0_attn_Wg': _L0_attn_in['Wg'], 'L0_attn_g_norm_w': _L0_attn_in['g_norm_w'], 'L0_attn_Wo': _L0_attn_in['Wo'], 'L0_ffn_Wr': _L0_ffn_in['Wr'], 'L0_ffn_W1': _L0_ffn_in['W1'], 'L0_ffn_W3': _L0_ffn_in['W3'], 'L0_ffn_W2': _L0_ffn_in['W2']}

def reference(x, txt, L0_tok_weight, L0_tok_weighted_sum, L0_attn_Wq, L0_attn_Wk, L0_attn_Wv, L0_attn_Wg1, L0_attn_Wg2, L0_attn_bg2, L0_attn_Wg, L0_attn_g_norm_w, L0_attn_Wo, L0_ffn_Wr, L0_ffn_W1, L0_ffn_W3, L0_ffn_W2):
    import jax
    import jax.numpy as jnp

    def _L0_tok_ref(x, weight, weighted_sum):
        import jax, jax.numpy as jnp
        import numpy as np
        return jnp.einsum('bhid,oi,od->bho', x, weighted_sum, weight)

    def _L0_attn_ref(x, Wq, Wk, Wv, Wg1, Wg2, bg2, Wg, g_norm_w, Wo):
        import jax, jax.numpy as jnp
        import numpy as np
        B, L, HID = (2, 512, 256)
        H = 16
        D = HID // H
        LR = 16
        EPS = 1e-05
        GLN = 16.0
        SCALE = D ** (-0.5)

        def _reference_tuple_inner(x, Wq, Wk, Wv, Wg1, Wg2, bg2, Wg, g_norm_w, Wo):
            Bb, Ll, Hid = x.shape
            q = (x @ Wq).reshape(Bb, Ll, H, D)
            k = (x @ Wk).reshape(Bb, Ll, H, D)
            v = (x @ Wv).reshape(Bb, Ll, H, D)
            gk = jax.nn.log_sigmoid(x @ Wg1 @ Wg2 + bg2).reshape(Bb, Ll, H, D) / GLN

            def step(S, inp):
                q_t, k_t, v_t, gk_t = inp
                S = jnp.exp(gk_t)[..., None] * S + k_t[..., None] * v_t[..., None, :]
                o_t = jnp.einsum('bhdv,bhd->bhv', S, q_t) * SCALE
                return (S, o_t)
            S0 = jnp.zeros((Bb, H, D, D), x.dtype)
            scan_in = tuple((jnp.moveaxis(t, 1, 0) for t in (q, k, v, gk)))
            S, o = jax.lax.scan(step, S0, scan_in)
            o = jnp.moveaxis(o, 0, 1)
            o = o * jax.lax.rsqrt(jnp.mean(o * o, axis=-1, keepdims=True) + EPS) * g_norm_w
            o = o.reshape(Bb, Ll, Hid)
            g = x @ Wg
            o = o * (g * jax.nn.sigmoid(g))
            o = o @ Wo
            return (o, S[:, None])
        return _reference_tuple_inner(x, Wq, Wk, Wv, Wg1, Wg2, bg2, Wg, g_norm_w, Wo)[0]

    def _L0_ffn_ref(x, Wr, W1, W3, W2):
        import math
        import jax, jax.numpy as jnp
        import numpy as np
        TOP_K = 2
        CAP_FACTOR = 1.25
        CLAMP = 10000.0
        B, S, D = x.shape
        E = Wr.shape[1]
        K = TOP_K
        T = B * S
        cap = max(1, math.ceil(T * K * CAP_FACTOR / E))
        xf = x.reshape(T, D)
        logits = jnp.clip(xf @ Wr, -CLAMP, CLAMP)
        top_v, top_i = jax.lax.top_k(logits, K)
        m = jnp.max(top_v, axis=-1, keepdims=True)
        expv = jnp.exp(top_v - m)
        top_p = expv / (jnp.sum(expv, axis=-1, keepdims=True) + 1e-12)
        Sp = T * K
        experts = top_i.reshape(Sp)
        weights = top_p.reshape(Sp)
        tokens = jnp.repeat(jnp.arange(T), K)
        oh = experts[:, None] == jnp.arange(E)[None, :]
        pos = jnp.sum(jnp.cumsum(oh.astype(jnp.int32), axis=0) * oh, axis=-1) - 1
        kept = pos < cap
        pos_safe = jnp.where(kept, pos, cap)
        xe = jnp.zeros((E, cap + 1, D), x.dtype).at[experts, pos_safe].set(xf[tokens])[:, :cap]
        h = jax.nn.silu(jnp.einsum('ecd,edf->ecf', xe, W1)) * jnp.einsum('ecd,edf->ecf', xe, W3)
        ye = jnp.einsum('ecf,efd->ecd', h, W2)
        yp = ye[experts, jnp.minimum(pos_safe, cap - 1)]
        wk = weights * kept.astype(weights.dtype)
        out = jnp.zeros((T, D), x.dtype).at[tokens].add(wk[:, None] * yp)
        return out.reshape(B, S, D)
    h = _L0_tok_ref(x, L0_tok_weight, L0_tok_weighted_sum)
    h = jnp.concatenate([h, txt], axis=1)
    h = h + _L0_attn_ref(_layernorm(h, axis=-1), L0_attn_Wq, L0_attn_Wk, L0_attn_Wv, L0_attn_Wg1, L0_attn_Wg2, L0_attn_bg2, L0_attn_Wg, L0_attn_g_norm_w, L0_attn_Wo)
    h = h + _L0_ffn_ref(_layernorm(h, axis=-1), L0_ffn_Wr, L0_ffn_W1, L0_ffn_W3, L0_ffn_W2)
    return h

_drawn_inputs = setup_inputs


def setup_inputs(seed=0):
    import zlib

    import numpy as np

    out = dict(_drawn_inputs(seed))
    spreads = {'L0_attn_bg2': (0.0, 0.8), 'L0_attn_g_norm_w': (1.0, 0.2)}
    factors = {'L0_attn_Wg1': 8.0, 'L0_attn_Wg2': 8.0}
    for name, (base, spread) in spreads.items():
        noise = np.random.default_rng([zlib.crc32(name.encode()), seed]).standard_normal(out[name].shape)
        drawn = base * np.exp(spread * noise) if base else spread * noise
        out[name] = jnp.asarray(drawn.astype(out[name].dtype))
    for name, factor in factors.items():
        out[name] = (out[name] * factor).astype(out[name].dtype)
    return out
```

```python
from contextlib import ExitStack

import numpy as np

import concourse.bass as bass
from concourse import mybir

F32 = mybir.dt.float32
F32R = mybir.dt.float32r
I32 = mybir.dt.int32
ALU = mybir.AluOpType
ACT = mybir.ActivationFunctionType
AX = mybir.AxisListType

P = 128
B, S, D, TX = 4, 512, 256, 32
DP = 4
L = S + TX
T = B * L
KD = D * DP
KT = KD // P
DT = D // P
H, HD = 16, 16
CH = [P] * (S // P) + [TX]
NC = len(CH)
ST = [P * c for c in range(NC)]
LP = P * NC
NW = L // 2
EPS = 1e-5
GLN = 16.0
QSCALE = HD ** -0.5
E, FF, TOPK = 8, 1024, 2
CAP = -(-T * TOPK * 5 // (4 * E))
FT = FF // P
TABLE = -(-(E * CAP + P) // P) * P
CLAMP = 10000.0
SPARE = 1 << (CAP - 1).bit_length()

EMBED = [("x_turn", 0, 0), ("x_turn", 0, 1)]
PROLOGUE = (
    [("load_x", 0), ("load_x", 1), ("load_txt",), ("x_turn", 0, 0), ("x_turn", 0, 1), ("load_x", 2),
     ("x_turn", 1, 0), ("x_turn", 1, 1), ("load_x", 3), ("embed", 0), ("ln1_stats", 0), ("ln1_rsqrt", 0),
     ("x_turn", 2, 0), ("x_turn", 2, 1), ("embed", 1), ("ln1_stats", 1), ("ln1_rsqrt", 1),
     ("ln1_apply", 0), ("x_turn", 3, 0), ("x_turn", 3, 1), ("embed", 2), ("ln1_stats", 2),
     ("ln1_rsqrt", 2), ("ln1_apply", 1), ("ln1_stats", 4), ("ln1_rsqrt", 4), ("ln1_apply", 4),
     ("xn_turn", 0), ("embed", 3), ("ln1_stats", 3), ("ln1_rsqrt", 3), ("ln1_apply", 2),
     ("xn_turn", 1), ("ln1_apply", 3), ("xn_turn", 2), ("xn_turn", 3), ("xn_turn", 4)]
)
NEXT = "next"
BODY = [
    ("hold_residual",), ("load_x", 0), ("load_x", 1), ("load_txt",),
    ("decay_proj", 0, 0), ("decay_proj", 0, 1), ("decay_proj", 1, 0), ("decay_proj", 1, 1),
    ("decay_abs", 0), ("v_proj", 0), ("v_proj", 1), ("decay_log", 0), ("decay_abs", 1), ("v_proj", 2),
    ("decay_log", 1), ("decay_sum", 0), ("v_proj", 3), ("v_proj", 4), ("decay_exp", 0),
    ("x_turn", 0, 0), ("x_turn", 0, 1), ("load_x", 2), ("decay_sum", 1), ("decay_exp", 1),
    ("x_turn", 1, 0), ("x_turn", 1, 1), ("load_x", 3), ("embed", 0),
    ("q_proj", 0, 0), ("q_proj", 0, 1), ("k_proj", 0, 0), ("k_proj", 0, 1), ("qk_split", 0),
    ("q_proj", 1, 0), ("q_proj", 1, 1), ("k_proj", 1, 0), ("k_proj", 1, 1), ("qk_split", 1),
    ("gate_proj", 0, 0), ("gate_proj", 0, 1), ("gate_proj", 1, 0), ("gate_proj", 1, 1),
    ("embed", 1), ("ln1_stats", 0),
    ("scores", 0), ("k_turn", 0), ("x_turn", 2, 0), ("x_turn", 2, 1), ("ln1_rsqrt", 0), ("ln1_stats", 1),
    ("scores", 1), ("state", 0), ("mix", 0), ("k_turn", 1), ("ln1_rsqrt", 1), ("ln1_apply", 0), ("embed", 2),
    ("scores", 2), ("state", 1), ("head_norm", 0), ("mix", 1), ("k_turn", 2), ("x_turn", 3, 0),
    ("x_turn", 3, 1), ("ln1_apply", 1), ("ln1_stats", 2), ("ln1_rsqrt", 2), ("attn_out", 0), ("ln2_stats", 0),
    ("scores", 3), ("state", 2), ("head_norm", 1), ("mix", 2), ("k_turn", 3), ("ln2_rsqrt", 0), ("embed", 3),
    ("ln1_apply", 2), ("ln1_stats", 3), ("ln1_rsqrt", 3), ("attn_out", 1), ("ln2_stats", 1), ("ln2_apply", 0),
    ("scores", 4), ("state", 3), ("head_norm", 2), ("mix", 3), ("xn2_turn", 0), ("ln2_rsqrt", 1),
    ("ln1_apply", 3), ("ln1_stats", 4), ("ln1_rsqrt", 4), ("attn_out", 2), ("ln2_stats", 2), ("ln2_apply", 1),
    ("router", 0), ("mix", 4), ("head_norm", 3), ("ln1_apply", 4), ("ln2_rsqrt", 2), ("xn2_turn", 1),
    ("xn_turn", 0), ("attn_out", 3), ("ln2_stats", 3), ("ln2_apply", 2), ("router", 1),
    ("head_norm", 4), ("ln2_rsqrt", 3), ("xn2_turn", 2), ("xn_turn", 1), ("attn_out", 4), ("ln2_stats", 4),
    ("ln2_apply", 3), ("router", 2), ("ln2_rsqrt", 4), ("xn2_turn", 3), ("xn_turn", 2), ("ln2_apply", 4),
    ("router", 3), ("xn_turn", 3), ("xn2_turn", 4), ("xn_turn", 4), ("router", 4),
    ("top2",), ("gate_exp",), ("rank",), ("slots",), ("table_scatter",),
]
FOR_NEXT = {"load_x", "load_txt", "x_turn", "embed", "ln1_stats", "ln1_rsqrt", "ln1_apply", "xn_turn"}
LAST = [s for s in BODY if s[0] not in FOR_NEXT]

CW = CAP // 2
TILES = [(h * CW + r, min(P, CW - r)) for h in range(2) for r in range(0, CW, P)]
NT = len(TILES)
HALF = FT // 2


def expert_body():
    steps = [("load_w13", 0), ("load_w2", 0), ("load_gather_index",), ("load_scatter_index",)]
    for f in range(FT):
        steps += [("up", f, 0)]
        if f:
            steps += [("h_split", f - 1, 1), ("w13_split", f - 1)]
            if f - 1 == HALF - 1:
                steps += [("load_w13", 1)]
        steps += [("w2_split", f)]
        if f == HALF - 1:
            steps += [("load_w2", 1)]
        if 1 <= f < 1 + NT:
            steps += [("gather", f - 1)]
        steps += [("up", f, 1), ("h_split", f, 0)]
    steps += [("h_split", FT - 1, 1), ("w13_split", FT - 1)]
    for n in range(NT):
        steps += [("down", n), ("scatter", n), ("xe_turn", n)]
    return steps + [("scattered",)]


EXPERT = expert_body()
EXPERT_AHEAD = [("load_w13", 0)] + [("w13_split", f) for f in range(HALF)] + [("load_w13", 1)] + \
               [("w13_split", f) for f in range(HALF, FT)]
EXPERT_FIRST = [("load_gather_index",)] + [("gather", n) for n in range(NT)] + [("xe_turn", n) for n in range(NT)]
EXPERT_PROLOGUE = EXPERT_AHEAD + EXPERT_FIRST
NEXT_EXPERT = {"load_w13", "w13_split", "load_gather_index", "gather", "xe_turn"}
LAST_EXPERT = [s for s in EXPERT if s[0] not in NEXT_EXPERT]
_at = LAST.index(("scores", 0))
LAST = LAST[:_at] + [EXPERT_AHEAD[0]] + LAST[_at:]
for _i, _s in enumerate(EXPERT_AHEAD[1:]):
    _at = LAST.index(("scores", 1)) + 6 + 5 * _i
    LAST.insert(_at, _s)

PROJ = ["decay_proj", "v_proj", "gate_proj", "q_proj", "k_proj"]
_n = 0
BANK = {}
for _s in BODY:
    if _s[0] in PROJ:
        BANK[_s] = _n % 4
        _n += 1
for _c in range(NC):
    BANK["mix", _c] = 4
    BANK["k_turn", _c] = 5
    BANK["state", _c] = 7
    BANK["head_norm", _c] = 5
    BANK["attn_out", _c] = 7
    BANK["xn2_turn", _c] = 5
    BANK["router", _c] = 7
    BANK["embed", _c] = (7, 5)[_c % 2]
    BANK["xn_turn", _c] = (5, 7)[_c % 2]
    for _q in range(2):
        BANK["x_turn", _c, _q] = 6
BANK["rank",] = 5
for _t in range(NT):
    BANK["down", _t] = 4 + _t % 2
    BANK["xe_turn", _t] = 6 + _t % 2
READER = {
    "x_turn": "dve", "embed": "act", "xn_turn": "dve", "decay_proj": "act", "v_proj": "act",
    "gate_proj": "act", "q_proj": "dve", "k_proj": "dve", "scores": "dve", "k_turn": "act",
    "state": "dve", "mix": "dve", "head_norm": "act", "attn_out": "dve", "xn2_turn": "act",
    "router": "dve", "rank": "dve", "up": "dve", "down": "dve", "xe_turn": "dve",
}
PARTS = {
    "load_x": {"sp": 16}, "load_txt": {"sp": 16}, "hold_residual": {"pool": 1},
    "x_turn": {"pe": 1, "act": 1, "dve": 1}, "embed": {"pe": 1, "act": 1},
    "ln1_stats": {"dve": 1}, "ln1_rsqrt": {"act": 1}, "ln1_apply": {"dve": 1},
    "xn_turn": {"pe": 1, "act": 1, "dve": 1},
    "decay_proj": {"pe": 1, "act": 1}, "decay_abs": {"dve": 1}, "decay_log": {"act": 1},
    "decay_sum": {"dve": 1}, "decay_exp": {"act": 1}, "v_proj": {"pe": 1, "act": 1},
    "gate_proj": {"pe": 1, "act": 1}, "q_proj": {"pe": 1, "dve": 1}, "k_proj": {"pe": 1, "dve": 1},
    "qk_split": {"act": 1, "dve": 1, "pool": 1},
    "scores": {"pe": 1, "dve": 1}, "k_turn": {"pe": 1, "act": 1}, "state": {"pe": 1, "dve": 1},
    "mix": {"pe": 1, "act": 1, "dve": 1}, "head_norm": {"pe": 1, "act": 1, "dve": 1},
    "attn_out": {"pe": 1, "dve": 1, "sp": 16},
    "ln2_stats": {"dve": 1}, "ln2_rsqrt": {"act": 1}, "ln2_apply": {"dve": 1, "sp": 16},
    "xn2_turn": {"pe": 1, "act": 1}, "router": {"pe": 1, "dve": 1},
    "top2": {"dve": 1}, "gate_exp": {"act": 1}, "rank": {"pe": 1}, "slots": {"dve": 1},
    "table_scatter": {"pool": 1},
    "load_w13": {"sp": 16}, "load_w2": {"sp": 16}, "load_gather_index": {"sp": 16},
    "load_scatter_index": {"sp": 16}, "gather": {"pool": 16},
    "w13_split": {"act": 1, "pool": 1}, "w2_split": {"act": 1, "pool": 1},
    "xe_turn": {"pe": 1, "act": 1, "dve": 1}, "up": {"pe": 1, "act": 1, "dve": 1},
    "h_split": {"act": 1, "dve": 1}, "down": {"pe": 1, "dve": 1}, "scatter": {}, "scattered": {"pool": 1},
}


INDEX_TRANSFERS = 2 * ((CW >= P) + (CW % P > 0))
TRANSFERS = {"load_w13": 2, "load_gather_index": INDEX_TRANSFERS, "load_scatter_index": INDEX_TRANSFERS}


def count_of(steps, kind):
    return sum(s[0] == kind for s in steps)


class Walk:

    def __init__(self, steps, i, prologue, body):
        self.steps, self.i, self.prologue, self.body = steps, i, prologue, body
        self.waited = {}

    def banks(self, step):
        if step[0] == "scores":
            return range(4)
        if step[0] == "up":
            return [2 * step[2], 2 * step[2] + 1]
        return [BANK[step]] if step in BANK else []

    def times(self, step, back=0):
        of_kind = [s for s in (self.prologue if self.i is None else self.body) if s[0] == step[0]]
        index = of_kind.index(step) + 1
        if self.i is None:
            return None if back else index
        per, before = count_of(self.body, step[0]), count_of(self.prologue, step[0])
        return (self.i - back) * per + (before or per) + index

    def before_in_bank(self, step, bank):
        own = self.steps if step in self.steps else self.prologue
        for other in reversed(own[:own.index(step)]):
            if bank in self.banks(other):
                return other, 0
        if self.i is None:
            return None, 0
        for other in reversed(self.body):
            if bank in self.banks(other):
                return other, 1
        return None, 0


def image(steps, b):
    return Walk(steps, b, PROLOGUE, BODY)


def expert(steps, e):
    return Walk(steps, e, EXPERT_PROLOGUE, EXPERT)


def fusion_kernel(nc, x, txt, tok_weight, tok_sum, wq, wk, wv, wg1, wg2, bg2, wg, g_norm, wo, wr, w1, w3, w2, out,
                  slot_table, xn_rows):
    ctx = ExitStack()
    with ctx:
        def sb(name, shape, dt=F32):
            return ctx.enter_context(nc.sbuf_tensor("sb_" + name, shape, dt))

        def sem(name):
            return ctx.enter_context(nc.semaphore(name))

        def psum(name):
            return ctx.enter_context(nc.psum_tensor(name, [P, 512], F32))

        RA = 4 * KT * P + 2 * KT * D + 10 * DT * D
        rarena = sb("rounded", [P, RA + 2 * FT * CAP + 2 * DT * CAP], F32R)
        at = [0]

        def rc(*shape):
            n = int(np.prod(shape))
            v = rarena[:, at[0]:at[0] + n]
            at[0] += n
            names = "abcdef"[:len(shape)]
            if len(shape) == 1:
                return v
            return v.rearrange(f"p ({' '.join(names)}) -> p {' '.join(names)}", **dict(zip(names, shape)))

        xt_hi, xt_lo = rc(2, KT, P), rc(2, KT, P)
        we_hi, we_lo = rc(KT, D), rc(KT, D)
        w5 = rc(5, 2, DT, D)
        xn_hi, xn_lo = rc(DT, LP), rc(DT, LP)
        q_hi, q_lo = rc(DT, 2, LP), rc(DT, 2, LP)
        k_hi, k_lo = rc(DT, LP), rc(DT, LP)

        at[0] = 0
        w13 = rc(FT, 2, 2, DT, P)
        w2s = rc(FT, 2, D)
        at[0] = 2 * 2 * KT * P + 2 * KT * D + 5 * 2 * DT * D
        h_hi, h_lo = rc(FT, CAP), rc(FT, CAP)
        xe_hi, xe_lo = rc(DT, CAP), rc(DT, CAP)
        x_in = sb("x_in", [P, 2, KD])
        h_new = sb("h_new", [P, NC, D])
        h_res = sb("h_res", [P, NC, D])
        xn = sb("xn", [P, NC, D])
        zq = sb("zq", [P, DT, L])
        gk = sb("gk", [P, DT, L])
        dec = sb("dec", [P, DT, L])
        gate = sb("gate", [P, DT, L])
        vp = sb("vp", [P, NC, 8, 3, HD])
        att = sb("att", [P, 2, 4, 4, P])
        kt = sb("kt", [P, 2, D])
        state = sb("state", [P, 2, DT, P])
        stmp = sb("stmp", [P, DT, P])
        sq = sb("sq", [P, 2, DT * P])
        rs = sb("rs", [P, DT * P])
        og = sb("og", [P, 2, DT, P])
        xn2 = sb("xn2", [P, NC, D])
        x2t = sb("x2t", [P, 2, DT, P])
        raw13 = sb("raw13", [P, 2048])
        raw2 = sb("raw2", [P, 1024])
        wo_sb = sb("wo", [P, DT, D])
        wr_sb = sb("wr", [P, DT, E])
        ident = sb("ident", [P, P])
        upper = sb("upper", [P, P])
        strict = sb("strict", [P, P])
        ones = sb("ones", [P, P])
        blocks = sb("blocks", [P, 8, HD])
        evenodd = sb("evenodd", [P, 2])
        tokw = sb("tokw", [P, DT, DP])
        bias = sb("bias", [P, DT])
        gnw = sb("gnw", [P, 1])
        eps = sb("eps", [P, 1])
        bn = sb("bn", [P, 2, 6])
        mv = sb("mv", [P, 2, NC, 2])
        ve = sb("ve", [P, 2, NC])
        y0 = sb("y0", [P, 2, NC])
        y1 = sb("y1", [P, 2, 4])
        lg = sb("lg", [P, NC, E])
        pick = sb("pick", [P, 2, NC, E])
        work = sb("work", [P, 2, NC, E])
        tops = sb("tops", [P, 4, NC])
        cum = sb("cum", [P, NC + 1, E])
        expert_no = sb("expert_no", [P, E])
        falling = sb("falling", [P, E])
        valid = sb("valid", [P, NC])
        dump = sb("dump", [P, NC])
        posk = sb("posk", [P, 4, 2, NC])
        token_no = sb("token_no", [P, NC])
        slot_of = sb("slot_of", [P, 2, NC], I32)
        rows = sb("rows", [P, 2, NC, 2])
        dummy = sb("dummy", [P, 1])
        tinit = sb("tinit", [P, TABLE // P, 2])
        tinit_i = sb("tinit_i", [P, TABLE // P], I32)

        att_flat = att[:, :, :, :, :].rearrange("p r j n t -> p (r j n t)")
        xe = att_flat[:, 0:NT * D].rearrange("p (n d) -> p n d", n=NT)
        ye = att_flat[:, NT * D:2 * NT * D].rearrange("p (n d) -> p n d", n=NT)
        gate_flat = gate[:, :, :].rearrange("p h t -> p (h t)")
        dec_flat = dec[:, :, :].rearrange("p h t -> p (h t)")
        g_index = sb("g_index", [P, NT, 2])
        s_index = sb("s_index", [P, NT, 2])
        prod = att[:, :, :, :, :].rearrange("p r j n t -> p (r j n t)")[:, 0:DT * KD].rearrange("p (h k) -> p h k", h=DT)

        ps = [psum(f"ps{i}") for i in range(8)]

        done = {(e, k): sem(f"{e}_{k}") for k, parts in PARTS.items() for e in parts
                if e != "sp" and k != "gather"}
        moved = {s: sem("_".join(map(str, s))) for s in BODY + EXPERT if "sp" in PARTS[s[0]] or s[0] == "gather"}
        ready = {n: sem(n) for n in (
            "weights_in", "consts_made", "product_made", "we_turned", "we_hi_made", "we_lo_made",
            "split_hi_made", "split_lo_made", "g1_turned", "g1_copied", "decay_w_made",
            "table_out", "table_rows_out", "rows_added", "zero_rows_out", "pads_zeroed", "settled")}
        chain = {e: sem(f"{e}_chain") for e in ("act", "dve", "pool")}

        def wait(eng, who, img, step, back=0):
            late = img.prologue if img.i is None else img.body
            mark = late.index(step) - back * len(late)
            key = (who, step if step in moved and who in ("sp", "pool") else step[0])
            if img.waited.get(key, -2 * len(late)) >= mark:
                return
            img.waited[key] = mark
            if step in moved and who in ("sp", "pool"):
                unit = 16 * TRANSFERS.get(step[0], 1)
                if img.i is not None:
                    eng.wait_ge(moved[step], (img.i - back + 2) * unit)
                elif not back:
                    eng.wait_ge(moved[step], unit)
                return
            n = img.times(step, back)
            if n is not None:
                eng.wait_ge(done[who, step[0]], n * PARTS[step[0]][who])

        def finish(ins, who, step):
            if step in moved and who in ("sp", "pool"):
                ins.then_inc(moved[step], 16)
            else:
                ins.then_inc(done[who, step[0]], PARTS[step[0]][who])

        class Chain:

            def __init__(self, who, eng):
                self.who, self.eng, self.base, self.n = who, eng, 0, 0

            def __call__(self, ins):
                self.n += 1
                ins.then_inc(chain[self.who], 1)
                self.eng.wait_ge(chain[self.who], self.base + self.n)

            def start(self, base):
                self.base, self.n = base, 0

        def settle(eng):
            eng.sem_inc(ready["settled"], 1)

        def first_wait_credit(eng, who):
            if who == "sp":
                for step, s in moved.items():
                    if step not in PROLOGUE + EXPERT_PROLOGUE:
                        eng.sem_inc(s, 16 * TRANSFERS.get(step[0], 1))
            for (e, k), s in done.items():
                if e == who and not count_of(PROLOGUE + EXPERT_PROLOGUE, k):
                    eng.sem_inc(s, count_of(BODY + EXPERT, k))

        def images(eng, walk, chained=None, per=0):
            walk(image(PROLOGUE, None))
            start = chained.base + chained.n if chained else 0
            with eng.Fori(0, B - 1) as b:
                if chained:
                    chained.start(b * per + start)
                walk(image(BODY, b))
                if chained:
                    assert chained.n == per, (chained.who, chained.n)
            if chained:
                chained.start((B - 1) * per + start)
            walk(image(LAST, B - 1))

        def bank_free(pe, img, step):
            for bank in img.banks(step):
                other, back = img.before_in_bank(step, bank)
                if other == ("rank",):
                    wait(pe, "dve", img, ("slots",), back)
                elif other is not None:
                    wait(pe, READER[other[0]], img, other, back)

        def experts(eng, walk):
            walk(expert(EXPERT_FIRST, None))
            with eng.Fori(0, E - 1) as e:
                walk(expert(EXPERT, e))
            walk(expert(LAST_EXPERT, E - 1))

        def attention_over(eng):
            last = image(LAST, B - 1)
            wait(eng, "pe", last, ("rank",))
            wait(eng, "dve", last, ("slots",))

        block = ctx.enter_context(nc.Block())

        x_tiles = x.rearrange("b (c p) i d -> (b c) p (i d)", p=P)
        out_rows = out
        CHN = S // P

        @block.sync
        def _(sp):
            w_in = ready["weights_in"]
            first_wait_credit(sp, "sp")
            loads = 0

            def load(dst, src, scattered=False):
                nonlocal loads
                sp.dma_start(dst, src, allow_slow_non_contiguous=scattered).then_inc(w_in, 16)
                loads += 1

            w13_in = [w.rearrange("e (k p) f -> e p k f", p=P) for w in (w1, w3)]
            w2_in = w2.rearrange("e (f p) d -> e p f d", p=P)
            table = slot_table
            ahead = expert(EXPERT_AHEAD, None)

            def expert_step(ex, s):
                kind, a = s[0], s[1:]
                this = 0 if ex.i is None else ex.i
                nxt = 0 if ex.i is None else ex.i + 1
                if kind == "load_w13":
                    prev = ("w13_split", FT - 1 if a[0] == 0 else HALF - 1)
                    wait(sp, "act", ex, prev, 1 - a[0])
                    wait(sp, "pool", ex, prev, 1 - a[0])
                    raw = raw13[:, :].rearrange("p (w k f) -> p w k f", w=2, k=DT)
                    cols = slice(a[0] * HALF * P, (a[0] + 1) * HALF * P)
                    for w in range(2):
                        sp.dma_start(raw[:, w, :, :], w13_in[w][nxt, :, :, cols]).then_inc(moved[s], 16)
                elif kind == "load_w2":
                    prev = ("w2_split", FT - 1 if a[0] == 0 else HALF - 1)
                    wait(sp, "act", ex, prev, 1 - a[0])
                    wait(sp, "pool", ex, prev, 1 - a[0])
                    finish(sp.dma_start(raw2[:, :].rearrange("p (f d) -> p f d", f=HALF),
                                        w2_in[this, :, a[0] * HALF:(a[0] + 1) * HALF, :]), "sp", s)
                elif kind in ("load_gather_index", "load_scatter_index"):
                    gathers = kind == "load_gather_index"
                    if gathers:
                        for n in range(NT):
                            wait(sp, "pool", ex, ("gather", n), 1)
                    else:
                        wait(sp, "pool", ex, ("scattered",), 1)
                        wait(sp, "dve", ex, ("down", NT - 1), 1)
                    dst = g_index if gathers else s_index
                    for h in range(2):
                        base = (nxt if gathers else this) * CAP + h * CW
                        n = CW // P
                        sp.dma_start(dst[:, h * NT // 2:h * NT // 2 + n, :],
                                     table[bass.ds(base, n * P), :].rearrange("(n p) t -> p n t", p=P)
                                     ).then_inc(moved[s], 16)
                        if CW % P:
                            sp.dma_start(dst[0:CW % P, h * NT // 2 + n, :],
                                         table[bass.ds(base + n * P, CW % P), :]).then_inc(moved[s], 16)

            def expert_steps(ex):
                for s in ex.steps:
                    if "sp" in PARTS[s[0]]:
                        expert_step(ex, s)

            def steps(img):
                nxt = 0 if img.i is None else img.i + 1
                for s in img.steps:
                    kind, a = s[0], s[1:]
                    if kind in NEXT_EXPERT:
                        expert_step(ahead, s)
                        continue
                    if kind == "load_x":
                        c = a[0]
                        prev = ("x_turn", c - 2, 1) if c >= 2 else ("x_turn", c + 2, 1)
                        wait(sp, "pe", img, prev, 0 if c >= 2 else 1)
                        finish(sp.dma_start(x_in[:, c % 2, :], x_tiles[nxt * CHN + c, :, :]), "sp", s)
                    elif kind == "load_txt":
                        if img.i is None:
                            sp.wait_ge(ready["pads_zeroed"], 1)
                        else:
                            wait(sp, "pool", img, ("hold_residual",))
                        finish(sp.dma_start(h_new[0:TX, NC - 1, :], txt[nxt, :, :]), "sp", s)
                    elif kind == "attn_out":
                        c = a[0]
                        wait(sp, "dve", img, s)
                        finish(sp.dma_start(out_rows[bass.ds(img.i * L + ST[c], CH[c]), :],
                                     h_res[0:CH[c], c, :]), "sp", s)
                    elif kind == "ln2_apply":
                        c = a[0]
                        wait(sp, "dve", img, s)
                        finish(sp.dma_start(xn_rows[bass.ds(img.i * L + ST[c], CH[c]), :],
                                     xn2[0:CH[c], c, :]), "sp", s)

            load(xn[:, 0:DT, :], tok_sum.rearrange("(h p) i -> p h i", p=P))
            load(tokw[:, :, :], tok_weight.rearrange("(h p) d -> p h d", p=P))
            for n, w in enumerate((wq, wk, wg, wv)):
                load(raw13[:, n * 512:(n + 1) * 512].rearrange("p (h o) -> p h o", h=DT),
                     w.rearrange("(h p) o -> p h o", p=P))
            load(raw2[:, 0:DT * HD].rearrange("p (h r) -> p h r", h=DT), wg1.rearrange("(h p) r -> p h r", p=P))
            load(raw2[0:HD, D:2 * D], wg2)
            load(wo_sb[:, :, :], wo.rearrange("(h p) o -> p h o", p=P))
            load(wr_sb[:, :, :], wr.rearrange("(h p) e -> p h e", p=P))
            load(bias[:, :], bg2.rearrange("(h p) -> p h", p=P), scattered=True)
            for n in range(P // HD):
                load(gnw[n * HD:(n + 1) * HD, :], g_norm.rearrange("(v a) -> v a", a=1), scattered=True)
            assert loads == WEIGHT_LOADS
            sp.wait_ge(ready["consts_made"], CONSTS)
            sp.wait_ge(ready["table_out"], 1)
            sp.dma_start(slot_table.rearrange("(p j) t -> p j t", p=P), tinit[:, :, :]).then_inc(ready["table_out"], 16)
            for dst in (xn_rows, out_rows):
                sp.dma_start(dst[T:T + SPARE, :].rearrange("(n p) d -> p n d", p=P),
                             kt[:, 0:1, :].to_broadcast([P, SPARE // P, D])).then_inc(ready["zero_rows_out"], 16)
            images(sp, steps)
            sp.wait_ge(ready["split_lo_made"], 5)
            attention_over(sp)
            wait(sp, "pool", image(LAST, B - 1), ("table_scatter",))
            experts(sp, expert_steps)
            sp.wait_ge(ready["rows_added"], 16 * NT * E)
            sp.wait_ge(ready["zero_rows_out"], 32)

        @block.gpsimd
        def _(pool):
            made = ready["consts_made"]
            first_wait_credit(pool, "pool")
            link = Chain("pool", pool)
            pool.memset(h_new[:, NC - 1, :], 0.0).then_inc(ready["pads_zeroed"], 1)
            link(pool.memset(ident[:, :], 0.0))
            pool.affine_select(out=ident[:, :], in_=ident[:, :], compare_op=ALU.not_equal, fill=1.0, base=0,
                               pattern=[[-1, P]], channel_multiplier=1).then_inc(made, 1)
            link(pool.memset(ones[:, :], 1.0))
            pool.affine_select(out=upper[:, :], in_=ones[:, :], compare_op=ALU.is_ge, fill=0.0, base=0,
                               pattern=[[1, P]], channel_multiplier=-1).then_inc(made, 1)
            pool.affine_select(out=strict[:, :], in_=ones[:, :], compare_op=ALU.is_gt, fill=0.0, base=0,
                               pattern=[[1, P]], channel_multiplier=-1).then_inc(made, 1)
            ones3 = ones[:, :].rearrange("p (n v) -> p n v", v=HD)
            link(pool.affine_select(out=blocks[:, :, :], in_=ones3, compare_op=ALU.is_ge, fill=0.0, base=0,
                                    pattern=[[-HD, P // HD], [0, HD]], channel_multiplier=1))
            pool.affine_select(out=blocks[:, :, :], in_=blocks[:, :, :], compare_op=ALU.is_ge, fill=0.0,
                               base=HD - 1, pattern=[[HD, P // HD], [0, HD]], channel_multiplier=-1).then_inc(made, 1)
            pool.memset(eps[:, :], EPS).then_inc(made, 1)
            pool.memset(kt[:, :, :], 0.0).then_inc(made, 1)
            pool.memset(vp[:, :, :, :, :], 0.0).then_inc(made, 1)
            pool.memset(lg[:, :, :], 0.0).then_inc(made, 1)
            pool.memset(cum[:, :, :], 0.0).then_inc(made, 1)
            pool.iota(expert_no[:, :], [[1, E]], base=0, channel_multiplier=0,
                      allow_small_or_imprecise_dtypes=True).then_inc(made, 1)
            pool.iota(falling[:, :], [[-1, E]], base=E, channel_multiplier=0,
                      allow_small_or_imprecise_dtypes=True).then_inc(made, 1)
            pool.iota(dump[:, :], [[0, NC]], base=E * CAP, channel_multiplier=1,
                      allow_small_or_imprecise_dtypes=True).then_inc(made, 1)
            pool.iota(token_no[:, :], [[P, NC]], base=-L, channel_multiplier=1,
                      allow_small_or_imprecise_dtypes=True).then_inc(made, 1)
            pool.iota(tinit_i[:, :], [[1, TABLE // P]], base=0, channel_multiplier=TABLE // P).then_inc(made, 1)
            link(pool.memset(valid[:, :], 1.0))
            pool.affine_select(out=valid[:, :], in_=valid[:, :], compare_op=ALU.is_gt, fill=0.0,
                               base=TX + (NC - 1) * P, pattern=[[-P, NC]], channel_multiplier=-1).then_inc(made, 1)
            pool.memset(xn_hi[:, :, L:LP].bitcast(F32), 0.0).then_inc(made, 1)
            pool.memset(xn_lo[:, :, L:LP].bitcast(F32), 0.0).then_inc(made, 1)
            pool.memset(k_hi[:, :, L:LP].bitcast(F32), 0.0).then_inc(made, 1)
            pool.memset(k_lo[:, :, L:LP].bitcast(F32), 0.0).then_inc(made, 1)
            pool.memset(tinit[:, :, 1:2], 0.0).then_inc(made, 1)

            ahead = expert(EXPERT_AHEAD, None)

            def expert_step(ex, s):
                kind, a = s[0], s[1:]
                if kind == "w13_split":
                    f = a[0]
                    wait(pool, "act", ex, s)
                    raw = raw13[:, :].rearrange("p (w k f) -> p w k f", w=2, k=DT)
                    cols = slice(f % HALF * P, (f % HALF + 1) * P)
                    for w in range(2):
                        ins = pool.tensor_tensor(w13[:, f, w, 1, :, :], raw[:, w, :, cols],
                                                 w13[:, f, w, 0, :, :].bitcast(F32), ALU.subtract)
                    finish(ins, "pool", s)
                elif kind == "w2_split":
                    f = a[0]
                    wait(pool, "act", ex, s)
                    finish(pool.tensor_tensor(w2s[:, f, 1, :], raw2[:, f % HALF * D:(f % HALF + 1) * D],
                                              w2s[:, f, 0, :].bitcast(F32), ALU.subtract), "pool", s)
                elif kind == "gather":
                    n = a[0]
                    wait(pool, "sp", ex, ("load_gather_index",))
                    wait(pool, "pe", ex, ("xe_turn", n), 1)
                    r = TILES[n][1]
                    settle(pool)
                    finish(pool.indirect_dma_start(
                        xe[0:r, n, :], None, xn_rows,
                        bass.IndirectOffsetOnAxis(ap=g_index[0:r, n, 0:1].bitcast(I32), axis=0)), "pool", s)
                elif kind == "scatter":
                    n = a[0]
                    wait(pool, "dve", ex, ("down", n))
                    r = TILES[n][1]
                    settle(pool)
                    pool.indirect_dma_start(
                        out_rows, bass.IndirectOffsetOnAxis(ap=s_index[0:r, n, 0:1].bitcast(I32), axis=0),
                        ye[0:r, n, :], None, compute_op=ALU.add).then_inc(ready["rows_added"], 16)
                elif kind == "scattered":
                    pool.wait_ge(ready["rows_added"], (ex.i + 1) * (16 * NT))
                    pool.sem_inc(done["pool", "scattered"], 1)

            def expert_steps(ex):
                for s in ex.steps:
                    if "pool" in PARTS[s[0]] or s[0] == "scatter":
                        expert_step(ex, s)

            def steps(img):
                for s in img.steps:
                    kind, a = s[0], s[1:]
                    if kind in NEXT_EXPERT:
                        expert_step(ahead, s)
                        continue
                    if kind == "hold_residual":
                        wait(pool, "dve", img, ("ln1_apply", 4), 1)
                        wait(pool, "act", img, ("embed", 3), 1)
                        for c in range(NC):
                            wait(pool, "sp", img, ("attn_out", c), 1)
                        wait(pool, "dve", img, ("attn_out", 4), 1)
                        wait(pool, "dve", img, ("ln2_apply", 4), 1)
                        settle(pool)
                        finish(pool.tensor_copy(h_res[:, :, :], h_new[:, :, :]), "pool", s)
                    elif kind == "qk_split":
                        hf = a[0]
                        wait(pool, "act", img, s)
                        wait(pool, "dve", img, ("k_proj", hf, 1))
                        wait(pool, "pe", img, ("scores", 4), 1)
                        finish(pool.tensor_tensor(k_lo[:, hf, 0:L], gk[:, hf, :],
                                                  k_hi[:, hf, 0:L].bitcast(F32), ALU.subtract), "pool", s)
                    elif kind == "table_scatter":
                        wait(pool, "dve", img, ("slots",))
                        settle(pool)
                        for c in range(NC):
                            for k in range(2):
                                pool.indirect_dma_start(
                                    slot_table, bass.IndirectOffsetOnAxis(ap=slot_of[0:CH[c], k, c:c + 1], axis=0),
                                    rows[0:CH[c], k, c, :], None).then_inc(ready["table_rows_out"], 16)
                        pool.wait_ge(ready["table_rows_out"], (img.i + 1) * (16 * 2 * NC))
                        pool.sem_inc(done["pool", "table_scatter"], 1)

            pool.wait_ge(ready["table_out"], 17)
            images(pool, steps)
            attention_over(pool)
            for c in range(NC):
                wait(pool, "sp", image(LAST, B - 1), ("ln2_apply", c))
                wait(pool, "sp", image(LAST, B - 1), ("attn_out", c))
            pool.wait_ge(ready["zero_rows_out"], 32)
            experts(pool, expert_steps)

        @block.scalar
        def _(act):
            first_wait_credit(act, "act")
            link = Chain("act", act)
            act.wait_ge(ready["weights_in"], 16 * WEIGHT_LOADS)
            for n in range(4):
                act.activation(w5[:, n + 1, 0, :, :], raw13[:, n * 512:(n + 1) * 512].rearrange("p (h o) -> p h o", h=DT),
                               ACT.Copy).then_inc(ready["split_hi_made"], 1)
            for n in range(4):
                act.wait_ge(ready["we_turned"], n + 1)
                act.activation(we_hi[:, 2 * n:2 * n + 2, :], ps[n][:, :].rearrange("p (k o) -> p k o", k=2),
                               ACT.Copy).then_inc(ready["we_hi_made"], 1)
            act.wait_ge(ready["g1_turned"], 1)
            act.activation(raw2[0:HD, 2 * D:3 * D], ps[4][0:HD, 0:D], ACT.Copy).then_inc(ready["g1_copied"], 1)
            act.wait_ge(ready["g1_turned"], 2)
            act.activation(w5[:, 0, 0, :, :], ps[5][:, :].rearrange("p (h o) -> p h o", h=DT),
                           ACT.Copy).then_inc(ready["split_hi_made"], 1)

            def rsqrt(s, img, m, c, who):
                r = CH[c]
                wait(act, "dve", img, (who, c))
                wait(act, "dve", img, ("ln1_apply" if m == 0 else "ln2_apply", c), 1)
                link(act.activation(y0[0:r, m, c:c + 1], ve[0:r, m, c:c + 1], ACT.Ln))
                finish(act.activation(y0[0:r, m, c:c + 1], y0[0:r, m, c:c + 1], ACT.Exp, scale=-0.5), "act", s)

            ahead = expert(EXPERT_AHEAD, None)

            def expert_step(ex, s):
                kind, a = s[0], s[1:]
                if kind == "w13_split":
                    f = a[0]
                    wait(act, "sp", ex, ("load_w13", f // HALF))
                    if ex.i is None:
                        wait(act, "pe", image(BODY, B - 2), ("embed", 3))
                    else:
                        wait(act, "pe", ex, ("up", f, 1))
                    raw = raw13[:, :].rearrange("p (w k f) -> p w k f", w=2, k=DT)
                    cols = slice(f % HALF * P, (f % HALF + 1) * P)
                    for w in range(2):
                        ins = act.activation(w13[:, f, w, 0, :, :], raw[:, w, :, cols], ACT.Copy)
                    finish(ins, "act", s)
                elif kind == "w2_split":
                    f = a[0]
                    wait(act, "sp", ex, ("load_w2", f // HALF))
                    wait(act, "pe", ex, ("down", NT - 1), 1)
                    finish(act.activation(w2s[:, f, 0, :], raw2[:, f % HALF * D:(f % HALF + 1) * D], ACT.Copy), "act", s)
                elif kind == "xe_turn":
                    n = a[0]
                    o, r = TILES[n]
                    wait(act, "pe", ex, s)
                    if ex.i is not None:
                        wait(act, "pe", ex, ("up", FT - 1, 1))
                    finish(act.activation(xe_hi[:, :, o:o + r], ps[BANK[s]][:, 0:DT * r].rearrange("p (h t) -> p h t", h=DT),
                                          ACT.Copy), "act", s)
                elif kind == "up":
                    f, h = a
                    wait(act, "pe", ex, s)
                    wait(act, "dve", ex, ("up", f - 1, h) if f else ("up", FT - 1, h), 0 if f else 1)
                    finish(act.activation(gate_flat[:, h * CW:(h + 1) * CW], ps[2 * h][:, 0:CW], ACT.Silu), "act", s)
                elif kind == "h_split":
                    f, h = a
                    wait(act, "dve", ex, ("up", f, h))
                    wait(act, "pe", ex, ("down", (h + 1) * NT // 2 - 1), 1)
                    finish(act.activation(h_hi[:, f, h * CW:(h + 1) * CW], dec_flat[:, h * CW:(h + 1) * CW], ACT.Copy),
                           "act", s)

            def expert_steps(ex):
                act.preload_act_table_set("silu_and_others")
                for s in ex.steps:
                    if "act" in PARTS[s[0]]:
                        expert_step(ex, s)

            def steps(img):
                act.preload_act_table_set("natural_log_exp_and_others")
                for s in img.steps:
                    kind, a = s[0], s[1:]
                    if kind in NEXT_EXPERT:
                        expert_step(ahead, s)
                        continue
                    if kind == "x_turn":
                        c, q = a
                        wait(act, "pe", img, s)
                        wait(act, "pe", img, ("embed", c - 2 if c >= 2 else c + 2), 0 if c >= 2 else 1)
                        finish(act.activation(xt_hi[:, c % 2, 4 * q:4 * q + 4, :],
                                              ps[6][:, :].rearrange("p (k t) -> p k t", k=4), ACT.Copy), "act", s)
                    elif kind == "embed":
                        c = a[0]
                        wait(act, "pe", img, s)
                        if img.i is not None:
                            wait(act, "pool", img, ("hold_residual",))
                        finish(act.activation(h_new[:, c, :], ps[BANK[s]][:, 0:D], ACT.Copy), "act", s)
                    elif kind == "ln1_rsqrt":
                        rsqrt(s, img, 0, a[0], "ln1_stats")
                    elif kind == "ln2_rsqrt":
                        rsqrt(s, img, 1, a[0], "ln2_stats")
                    elif kind == "xn_turn":
                        c = a[0]
                        r = CH[c]
                        wait(act, "pe", img, s)
                        if img.i is not None:
                            wait(act, "pe", img, ("gate_proj", 1, 1))
                            wait(act, "pe", img, ("k_proj", 1, 1))
                        finish(act.activation(xn_hi[:, :, ST[c]:ST[c] + r],
                                              ps[BANK[s]][:, 0:DT * r].rearrange("p (h t) -> p h t", h=DT),
                                              ACT.Copy), "act", s)
                    elif kind == "decay_proj":
                        hf, n = a
                        wait(act, "pe", img, s)
                        wait(act, "pe", img, ("mix", 4), 1)
                        wait(act, "dve", img, ("qk_split", 1), 1)
                        wait(act, "act", img, ("qk_split", 1), 1)
                        finish(act.activation(zq[:, hf, n * NW:(n + 1) * NW], ps[BANK[s]][:, 0:NW], ACT.Identity,
                                              bias=bias[:, hf:hf + 1]), "act", s)
                    elif kind == "decay_log":
                        hf = a[0]
                        wait(act, "dve", img, ("decay_abs", hf))
                        link(act.activation(gk[:, hf, :], gk[:, hf, :], ACT.Exp))
                        finish(act.activation(gk[:, hf, :], gk[:, hf, :], ACT.Ln, bias=ones[:, 0:1]), "act", s)
                    elif kind == "decay_exp":
                        hf = a[0]
                        wait(act, "dve", img, ("decay_sum", hf))
                        wait(act, "dve", img, ("state", 3), 1)
                        act.activation(dec[:, hf, :], gk[:, hf, :], ACT.Exp, scale=1.0 / GLN)
                        finish(act.activation(gk[:, hf, :], gk[:, hf, :], ACT.Exp, scale=-1.0 / GLN), "act", s)
                    elif kind == "v_proj":
                        c = a[0]
                        r = CH[c]
                        wait(act, "pe", img, s)
                        wait(act, "pe", img, ("mix", c), 1)
                        finish(act.activation(vp[0:r, c, :, 0:3:2, :],
                                              ps[BANK[s]][0:r, 0:D].rearrange("p (n e v) -> p n e v", e=2, v=HD),
                                              ACT.Copy), "act", s)
                    elif kind == "gate_proj":
                        hf, n = a
                        wait(act, "pe", img, s)
                        wait(act, "dve", img, ("mix", 4), 1)
                        finish(act.activation(gate[:, hf, n * NW:(n + 1) * NW], ps[BANK[s]][:, 0:NW], ACT.Silu), "act", s)
                        if a == (1, 1):
                            act.preload_act_table_set("natural_log_exp_and_others")
                    elif kind == "qk_split":
                        hf = a[0]
                        wait(act, "dve", img, ("q_proj", hf, 1))
                        wait(act, "dve", img, ("k_proj", hf, 1))
                        wait(act, "pe", img, ("scores", 4), 1)
                        for e in range(2):
                            act.activation(q_hi[:, hf, e, 0:L], zq[:, hf, :], ACT.Copy, scale=evenodd[:, e:e + 1])
                        finish(act.activation(k_hi[:, hf, 0:L], gk[:, hf, :], ACT.Copy), "act", s)
                    elif kind == "k_turn":
                        c = a[0]
                        wait(act, "pe", img, s)
                        prev = ("state", c - 2) if c >= 2 else ("state", c + 2)
                        wait(act, "pe", img, prev, 0 if c >= 2 else 1)
                        finish(act.activation(kt[:, c % 2, :], ps[BANK[s]][:, 0:D], ACT.Copy), "act", s)
                    elif kind == "mix":
                        c = a[0]
                        w = DT * CH[c]
                        wait(act, "pe", img, s)
                        wait(act, "pe", img, ("head_norm", c - 2) if c >= 2 else ("head_norm", 4), 0 if c >= 2 else 1)
                        finish(act.activation(sq[:, c % 2, 0:w], ps[4][:, 0:w], ACT.Square), "act", s)
                    elif kind == "head_norm":
                        c = a[0]
                        w = DT * CH[c]
                        wait(act, "pe", img, s)
                        wait(act, "dve", img, ("head_norm", c - 1) if c else ("head_norm", 4), 0 if c else 1)
                        link(act.activation(rs[:, 0:w], ps[BANK[s]][:, 0:w], ACT.Ln, bias=eps[:, 0:1], scale=1.0 / HD))
                        finish(act.activation(rs[:, 0:w], rs[:, 0:w], ACT.Exp, scale=-0.5), "act", s)
                    elif kind == "xn2_turn":
                        c = a[0]
                        r = CH[c]
                        wait(act, "pe", img, s)
                        wait(act, "pe", img, ("router", c - 2) if c >= 2 else ("router", 4), 0 if c >= 2 else 1)
                        finish(act.activation(x2t[:, c % 2, :, 0:r],
                                              ps[BANK[s]][:, 0:DT * r].rearrange("p (h t) -> p h t", h=DT),
                                              ACT.Copy), "act", s)
                    elif kind == "gate_exp":
                        wait(act, "dve", img, ("top2",))
                        finish(act.activation(tops[:, 2, :], tops[:, 2, :], ACT.Exp), "act", s)

            act.wait_ge(ready["consts_made"], CONSTS)
            images(act, steps, link, ACT_CHAIN)
            attention_over(act)
            experts(act, expert_steps)

        @block.vector
        def _(dve):
            first_wait_credit(dve, "dve")
            link = Chain("dve", dve)
            dve.wait_ge(ready["consts_made"], CONSTS)
            dve.wait_ge(ready["weights_in"], 16 * WEIGHT_LOADS)
            dve.tensor_reduce(evenodd[:, 0:1], blocks[:, 0:8:2, 0:1], AX.XY, ALU.add).then_inc(ready["product_made"], 1)
            dve.tensor_reduce(evenodd[:, 1:2], blocks[:, 1:8:2, 0:1], AX.XY, ALU.add).then_inc(ready["product_made"], 1)
            for hf in range(DT):
                dve.tensor_tensor(
                    prod[:, hf, :].rearrange("p (i d) -> p i d", d=DP),
                    xn[:, hf, :].rearrange("p (i a) -> p i a", a=1).to_broadcast([P, D, DP]),
                    tokw[:, hf:hf + 1, :].to_broadcast([P, D, DP]), ALU.mult).then_inc(ready["product_made"], 1)
            link(dve.tensor_scalar(tinit_i[:, :], tinit_i[:, :], SPARE - 1, None, ALU.bitwise_and))
            link(dve.tensor_copy(tinit[:, :, 0], tinit_i[:, :]))
            link(dve.tensor_scalar(tinit[:, :, 0], tinit[:, :, 0], float(T), None, ALU.add))
            dve.tensor_copy(tinit[:, :, 0].bitcast(I32), tinit[:, :, 0]).then_inc(ready["table_out"], 1)
            for n in range(4):
                dve.wait_ge(ready["split_hi_made"], n + 1)
                dve.tensor_tensor(w5[:, n + 1, 1, :, :], raw13[:, n * 512:(n + 1) * 512].rearrange("p (h o) -> p h o", h=DT),
                                  w5[:, n + 1, 0, :, :].bitcast(F32), ALU.subtract).then_inc(ready["split_lo_made"], 1)
            for n in range(4):
                dve.wait_ge(ready["we_hi_made"], n + 1)
                dve.tensor_tensor(we_lo[:, 2 * n:2 * n + 2, :], ps[n][:, :].rearrange("p (k o) -> p k o", k=2),
                                  we_hi[:, 2 * n:2 * n + 2, :].bitcast(F32), ALU.subtract).then_inc(ready["we_lo_made"], 1)
            dve.wait_ge(ready["split_hi_made"], 5)
            dve.tensor_tensor(w5[:, 0, 1, :, :], ps[5][:, :].rearrange("p (h o) -> p h o", h=DT),
                              w5[:, 0, 0, :, :].bitcast(F32), ALU.subtract).then_inc(ready["split_lo_made"], 1)

            def stats(s, src, m, c):
                r = CH[c]
                link(dve.bn_stats(bn[0:r, m, :], src[0:r, c, :]))
                settle(dve)
                link(dve.bn_aggr(mv[0:r, m, c, :], bn[0:r, m, :]))
                finish(dve.tensor_scalar(ve[0:r, m, c:c + 1], mv[0:r, m, c, 1:2], EPS, None, ALU.add), "dve", s)

            def normalise(s, dst, src, m, c):
                r = CH[c]
                y, v, t = y0[0:r, m, c:c + 1], ve[0:r, m, c:c + 1], y1[0:r, m, :]
                link(dve.scalar_tensor_tensor(t[:, 0:1], y, y, v, ALU.mult, ALU.mult))
                link(dve.tensor_scalar(t[:, 1:2], t[:, 0:1], -0.5, 1.5, ALU.mult, ALU.add))
                link(dve.tensor_tensor(t[:, 2:3], y, t[:, 1:2], ALU.mult))
                finish(dve.tensor_scalar(dst[0:r, c, :], src[0:r, c, :], mv[0:r, m, c, 0:1], t[:, 2:3],
                                         ALU.subtract, ALU.mult), "dve", s)

            ahead = expert(EXPERT_AHEAD, None)

            def expert_step(ex, s):
                kind, a = s[0], s[1:]
                if kind == "xe_turn":
                    n = a[0]
                    o, r = TILES[n]
                    wait(dve, "act", ex, s)
                    finish(dve.tensor_tensor(xe_lo[:, :, o:o + r],
                                             ps[BANK[s]][:, 0:DT * r].rearrange("p (h t) -> p h t", h=DT),
                                             xe_hi[:, :, o:o + r].bitcast(F32), ALU.subtract), "dve", s)
                elif kind == "up":
                    f, h = a
                    wait(dve, "act", ex, s)
                    wait(dve, "dve", ex, ("h_split", f - 1, h) if f else ("h_split", FT - 1, h), 0 if f else 1)
                    cols = slice(h * CW, (h + 1) * CW)
                    finish(dve.tensor_tensor(dec_flat[:, cols], ps[2 * h + 1][:, 0:CW], gate_flat[:, cols], ALU.mult),
                           "dve", s)
                elif kind == "h_split":
                    f, h = a
                    wait(dve, "act", ex, s)
                    cols = slice(h * CW, (h + 1) * CW)
                    finish(dve.tensor_tensor(h_lo[:, f, cols], dec_flat[:, cols], h_hi[:, f, cols].bitcast(F32),
                                             ALU.subtract), "dve", s)
                elif kind == "down":
                    n = a[0]
                    r = TILES[n][1]
                    wait(dve, "pe", ex, s)
                    wait(dve, "sp", ex, ("load_scatter_index",))
                    wait(dve, "pool", ex, ("scattered",), 1)
                    finish(dve.tensor_scalar(ye[0:r, n, :], ps[BANK[s]][0:r, 0:D], s_index[0:r, n, 1:2], None,
                                             ALU.mult), "dve", s)

            def expert_steps(ex):
                for s in ex.steps:
                    if "dve" in PARTS[s[0]]:
                        expert_step(ex, s)

            def steps(img):
                for s in img.steps:
                    kind, a = s[0], s[1:]
                    if kind in NEXT_EXPERT:
                        expert_step(ahead, s)
                        continue
                    if kind == "x_turn":
                        c, q = a
                        wait(dve, "act", img, s)
                        finish(dve.tensor_tensor(xt_lo[:, c % 2, 4 * q:4 * q + 4, :],
                                                 ps[6][:, :].rearrange("p (k t) -> p k t", k=4),
                                                 xt_hi[:, c % 2, 4 * q:4 * q + 4, :].bitcast(F32), ALU.subtract), "dve", s)
                    elif kind == "ln1_stats":
                        c = a[0]
                        if c < NC - 1:
                            wait(dve, "act", img, ("embed", c))
                        else:
                            wait(dve, "sp", img, ("load_txt",))
                        stats(s, h_new, 0, c)
                    elif kind == "ln1_apply":
                        c = a[0]
                        wait(dve, "act", img, ("ln1_rsqrt", c))
                        wait(dve, "pe", img, ("xn_turn", c), 1)
                        normalise(s, xn, h_new, 0, c)
                    elif kind == "ln2_stats":
                        wait(dve, "dve", img, ("attn_out", a[0]))
                        stats(s, h_res, 1, a[0])
                    elif kind == "ln2_apply":
                        c = a[0]
                        wait(dve, "act", img, ("ln2_rsqrt", c))
                        wait(dve, "pe", img, ("xn2_turn", c), 1)
                        wait(dve, "sp", img, s, 1)
                        normalise(s, xn2, h_res, 1, c)
                    elif kind == "xn_turn":
                        c = a[0]
                        r = CH[c]
                        wait(dve, "act", img, s)
                        finish(dve.tensor_tensor(xn_lo[:, :, ST[c]:ST[c] + r],
                                                 ps[BANK[s]][:, 0:DT * r].rearrange("p (h t) -> p h t", h=DT),
                                                 xn_hi[:, :, ST[c]:ST[c] + r].bitcast(F32), ALU.subtract), "dve", s)
                    elif kind == "decay_abs":
                        hf = a[0]
                        wait(dve, "act", img, ("decay_proj", hf, 1))
                        wait(dve, "pe", img, ("k_turn", 3), 1)
                        wait(dve, "act", img, ("qk_split", 1), 1)
                        wait(dve, "pool", img, ("qk_split", 1), 1)
                        finish(dve.scalar_tensor_tensor(gk[:, hf, :], zq[:, hf, :], -1.0, zq[:, hf, :],
                                                        ALU.mult, ALU.min), "dve", s)
                    elif kind == "decay_sum":
                        hf = a[0]
                        wait(dve, "act", img, ("decay_log", hf))
                        link(dve.scalar_tensor_tensor(zq[:, hf, :], zq[:, hf, :], 0.0, gk[:, hf, :],
                                                      ALU.min, ALU.subtract))
                        for c in range(NC):
                            at_c = slice(ST[c], ST[c] + CH[c])
                            ins = dve.tensor_tensor_scan(gk[:, hf, at_c], ones[:, 0:CH[c]], zq[:, hf, at_c], 0.0,
                                                         ALU.mult, ALU.add)
                        finish(ins, "dve", s)
                    elif kind == "q_proj":
                        hf, n = a
                        w = slice(n * NW, (n + 1) * NW)
                        wait(dve, "pe", img, s)
                        wait(dve, "act", img, ("decay_exp", hf))
                        finish(dve.scalar_tensor_tensor(zq[:, hf, w], ps[BANK[s]][:, 0:NW], QSCALE, dec[:, hf, w],
                                                        ALU.mult, ALU.mult), "dve", s)
                    elif kind == "k_proj":
                        hf, n = a
                        w = slice(n * NW, (n + 1) * NW)
                        wait(dve, "pe", img, s)
                        wait(dve, "act", img, ("decay_exp", hf))
                        finish(dve.tensor_tensor(gk[:, hf, w], ps[BANK[s]][:, 0:NW], gk[:, hf, w], ALU.mult), "dve", s)
                    elif kind == "qk_split":
                        hf = a[0]
                        wait(dve, "act", img, s)
                        wait(dve, "dve", img, ("q_proj", hf, 1))
                        for e in range(2):
                            ins = dve.scalar_tensor_tensor(q_lo[:, hf, e, 0:L], zq[:, hf, :], evenodd[:, e:e + 1],
                                                           q_hi[:, hf, e, 0:L].bitcast(F32), ALU.mult, ALU.subtract)
                        finish(ins, "dve", s)
                    elif kind == "scores":
                        c = a[0]
                        r = CH[c]
                        wait(dve, "pe", img, s)
                        wait(dve, "pe", img, ("mix", c - 2) if c >= 2 else ("mix", 4), 0 if c >= 2 else 1)
                        for j in range(4):
                            ins = dve.tensor_tensor(att[0:r, c % 2, j, :, 0:r],
                                                    ps[j][0:r, 0:4 * r].rearrange("p (n t) -> p n t", n=4),
                                                    upper[0:r, 0:r].rearrange("p (a t) -> p a t", a=1)
                                                    .to_broadcast([r, 4, r]), ALU.mult)
                        finish(ins, "dve", s)
                    elif kind == "state":
                        c = a[0]
                        wait(dve, "pe", img, s)
                        if c >= 1:
                            wait(dve, "pe", img, ("mix", c - 1))
                        else:
                            wait(dve, "pe", img, ("mix", 4), 1)
                        end = ST[c] + P - 1
                        for hf in range(DT):
                            dst = state[:, (c + 1) % 2, hf, :] if c == 0 else stmp[:, hf, :]
                            ins = dve.scalar_tensor_tensor(dst, ps[BANK[s]][:, hf * P:(hf + 1) * P],
                                                           dec[:, hf, end:end + 1],
                                                           blocks[:, :, :].rearrange("p n v -> p (n v)"),
                                                           ALU.mult, ALU.mult)
                            if c:
                                link(ins)
                                ins = dve.scalar_tensor_tensor(state[:, (c + 1) % 2, hf, :], state[:, c % 2, hf, :],
                                                               dec[:, hf, end:end + 1], stmp[:, hf, :],
                                                               ALU.mult, ALU.add)
                        finish(ins, "dve", s)
                    elif kind == "mix":
                        c = a[0]
                        r = CH[c]
                        wait(dve, "act", img, s)
                        wait(dve, "act", img, ("gate_proj", 1, 1))
                        wait(dve, "pe", img, ("attn_out", c - 2) if c >= 2 else ("attn_out", 4), 0 if c >= 2 else 1)
                        finish(dve.scalar_tensor_tensor(og[:, c % 2, :, 0:r],
                                                        ps[4][:, 0:DT * r].rearrange("p (h t) -> p h t", h=DT),
                                                        gnw[:, 0:1], gate[:, :, ST[c]:ST[c] + r],
                                                        ALU.mult, ALU.mult), "dve", s)
                    elif kind == "head_norm":
                        c = a[0]
                        r = CH[c]
                        wait(dve, "act", img, s)
                        wait(dve, "dve", img, ("mix", c))
                        finish(dve.tensor_tensor(og[:, c % 2, :, 0:r], og[:, c % 2, :, 0:r],
                                                 rs[:, 0:DT * r].rearrange("p (h t) -> p h t", h=DT), ALU.mult), "dve", s)
                    elif kind == "attn_out":
                        c = a[0]
                        r = CH[c]
                        wait(dve, "pe", img, s)
                        wait(dve, "pool", img, ("hold_residual",))
                        finish(dve.tensor_tensor(h_res[0:r, c, :], ps[BANK[s]][0:r, 0:D], h_res[0:r, c, :], ALU.add),
                               "dve", s)
                    elif kind == "router":
                        c = a[0]
                        r = CH[c]
                        wait(dve, "pe", img, s)
                        finish(dve.tensor_scalar(lg[0:r, c, :], ps[BANK[s]][0:r, 0:E], CLAMP, -CLAMP, ALU.min, ALU.max),
                               "dve", s)
                    elif kind == "top2":
                        wait(dve, "dve", img, ("router", 4))
                        wait(dve, "dve", img, ("slots",), 1)
                        wait(dve, "pe", img, ("rank",), 1)
                        wait(dve, "pool", img, ("table_scatter",), 1)

                        def over_experts(v):
                            return v.rearrange("p (c a) -> p c a", a=1).to_broadcast([P, NC, E])

                        fall = falling[:, :].rearrange("p (a e) -> p a e", a=1).to_broadcast([P, NC, E])
                        link(dve.tensor_scalar(token_no[:, :], token_no[:, :], float(L), None, ALU.add))
                        src = lg[:, :, :]
                        for k in range(2):
                            link(dve.tensor_reduce(tops[:, k, :], src, AX.X, ALU.max))
                            link(dve.tensor_tensor(work[:, 0], src, over_experts(tops[:, k, :]), ALU.is_equal))
                            link(dve.tensor_tensor(work[:, 0], work[:, 0], fall, ALU.mult))
                            link(dve.tensor_reduce(tops[:, 3, :], work[:, 0], AX.X, ALU.max))
                            link(dve.tensor_tensor(pick[:, k], work[:, 0], over_experts(tops[:, 3, :]), ALU.is_equal))
                            if k == 0:
                                link(dve.scalar_tensor_tensor(work[:, 1], pick[:, 0], -3.0e38, lg[:, :, :],
                                                              ALU.mult, ALU.add))
                                src = work[:, 1]
                        link(dve.tensor_tensor(tops[:, 2, :], tops[:, 1, :], tops[:, 0, :], ALU.subtract))
                        link(dve.tensor_tensor(work[:, 0], pick[:, 0], pick[:, 1], ALU.add))
                        link(dve.tensor_tensor(work[:, 0], work[:, 0], over_experts(valid[:, :]), ALU.mult))
                        link(dve.tensor_copy(cum[:, 0, :], cum[:, NC, :]))
                        for c in range(NC):
                            ins = dve.tensor_tensor(cum[:, c + 1, :], cum[:, c, :], work[:, 0, c, :], ALU.add)
                            if c < NC - 1:
                                link(ins)
                        finish(ins, "dve", s)
                    elif kind == "slots":
                        wait(dve, "act", img, ("gate_exp",))
                        w1k, w2k = tops[:, 0, :], tops[:, 1, :]
                        link(dve.tensor_scalar(w1k, tops[:, 2, :], 1.0, 1e-12, ALU.add, ALU.add))
                        link(dve.reciprocal(w1k, w1k))
                        link(dve.tensor_tensor(w2k, tops[:, 2, :], w1k, ALU.mult))
                        for k in range(2):
                            dve.tensor_copy(rows[:, k, :, 1], tops[:, k, :])
                            dve.tensor_copy(rows[:, k, :, 0].bitcast(I32), token_no[:, :])
                        wait(dve, "pe", img, ("rank",))
                        rank = ps[BANK["rank",]][:, 0:NC * E].rearrange("p (c e) -> p c e", c=NC)
                        eno = expert_no[:, :].rearrange("p (a e) -> p a e", a=1).to_broadcast([P, NC, E])
                        for k in range(2):
                            link(dve.tensor_tensor(work[:, 1], rank, pick[:, k], ALU.mult))
                            link(dve.tensor_reduce(posk[:, 0, k, :], work[:, 1], AX.X, ALU.add))
                            link(dve.tensor_tensor(work[:, 1], pick[:, k], eno, ALU.mult))
                            link(dve.tensor_reduce(posk[:, 1, k, :], work[:, 1], AX.X, ALU.add))
                            link(dve.tensor_scalar(posk[:, 2, k, :], posk[:, 0, k, :], float(CAP), None, ALU.is_lt))
                            link(dve.scalar_tensor_tensor(posk[:, 1, k, :], posk[:, 1, k, :], float(CAP),
                                                          posk[:, 0, k, :], ALU.mult, ALU.add))
                            link(dve.tensor_tensor(posk[:, 1, k, :], posk[:, 1, k, :], dump[:, :], ALU.subtract))
                            link(dve.tensor_tensor(posk[:, 1, k, :], posk[:, 1, k, :], posk[:, 2, k, :], ALU.mult))
                            link(dve.tensor_tensor(posk[:, 1, k, :], posk[:, 1, k, :], dump[:, :], ALU.add))
                            ins = dve.tensor_copy(slot_of[:, k, :], posk[:, 1, k, :])
                            if k == 0:
                                link(ins)
                        finish(ins, "dve", s)

            dve.wait_ge(ready["pads_zeroed"], 1)
            images(dve, steps, link, DVE_CHAIN)
            attention_over(dve)
            experts(dve, expert_steps)

        @block.tensor
        def _(pe):
            first_wait_credit(pe, "pe")
            pe.wait_ge(ready["product_made"], 4)
            pe.wait_ge(ready["consts_made"], CONSTS)
            for n in range(4):
                for kk in range(2):
                    for hf in range(DT):
                        ins = pe.transpose(ps[n][:, (2 * kk + hf) * P:(2 * kk + hf + 1) * P],
                                           prod[:, hf, (2 * n + kk) * P:(2 * n + kk + 1) * P], ident[:, :])
                ins.then_inc(ready["we_turned"], 1)
            pe.wait_ge(ready["weights_in"], 16 * WEIGHT_LOADS)
            for hf in range(DT):
                ins = pe.matmul(ps[4][0:HD, hf * P:(hf + 1) * P], raw2[:, hf * HD:(hf + 1) * HD], ident[:, :],
                                start=True, stop=True)
            ins.then_inc(ready["g1_turned"], 1)
            pe.wait_ge(ready["g1_copied"], 1)
            for hf in range(DT):
                ins = pe.matmul(ps[5][:, hf * D:(hf + 1) * D], raw2[0:HD, 2 * D + hf * P:2 * D + (hf + 1) * P],
                                raw2[0:HD, D:2 * D], start=True, stop=True)
            ins.then_inc(ready["g1_turned"], 1)
            pe.wait_ge(ready["we_lo_made"], 4)
            pe.wait_ge(ready["split_lo_made"], 5)

            def three(out_ap, pairs):
                n = 3 * len(pairs)
                i = 0
                for (a_hi, a_lo), (b_hi, b_lo) in pairs:
                    for lhs, rhs in ((a_hi, b_hi), (a_hi, b_lo), (a_lo, b_hi)):
                        ins = pe.matmul(out_ap, lhs, rhs, start=(i == 0), stop=(i == n - 1))
                        i += 1
                return ins

            ahead = expert(EXPERT_AHEAD, None)

            def expert_step(ex, s):
                kind, a = s[0], s[1:]
                bank_free(pe, ex, s)
                if kind == "xe_turn":
                    n = a[0]
                    r = TILES[n][1]
                    wait(pe, "pool", ex, ("gather", n))
                    for hf in range(DT):
                        ins = pe.transpose(ps[BANK[s]][:, hf * r:(hf + 1) * r], xe[0:r, n, hf * P:(hf + 1) * P],
                                           ident[0:r, 0:r])
                    finish(ins, "pe", s)
                elif kind == "up":
                    f, h = a
                    wait(pe, "pool", ex, ("w13_split", f), 1)
                    wait(pe, "dve", ex, ("xe_turn", (h + 1) * NT // 2 - 1), 1)
                    cols = slice(h * CW, (h + 1) * CW)
                    for w in range(2):
                        ins = three(ps[2 * h + w][:, 0:CW], [((w13[:, f, w, 0, k, :], w13[:, f, w, 1, k, :]),
                                                              (xe_hi[:, k, cols], xe_lo[:, k, cols])) for k in range(DT)])
                    finish(ins, "pe", s)
                elif kind == "down":
                    n = a[0]
                    o, r = TILES[n]
                    h = o // CW
                    wait(pe, "pool", ex, ("w2_split", FT - 1))
                    for f in range(FT):
                        if f == FT - 1:
                            wait(pe, "dve", ex, ("h_split", f, h))
                        elif f == 0:
                            wait(pe, "dve", ex, ("h_split", FT - 2, h))
                        for i, (hh, ww) in enumerate(((h_hi, 0), (h_hi, 1), (h_lo, 0))):
                            ins = pe.matmul(ps[BANK[s]][0:r, 0:D], hh[:, f, o:o + r], w2s[:, f, ww, :],
                                            start=(f == 0 and i == 0), stop=(f == FT - 1 and i == 2))
                    finish(ins, "pe", s)

            def expert_steps(ex):
                for s in ex.steps:
                    if "pe" in PARTS[s[0]]:
                        expert_step(ex, s)

            def steps(img):
                for s in img.steps:
                    kind, a = s[0], s[1:]
                    if kind in NEXT_EXPERT:
                        expert_step(ahead, s)
                        continue
                    if "pe" in PARTS[kind] :
                        bank_free(pe, img, s)
                    bank = ps[BANK[s]] if s in BANK else None
                    if kind == "x_turn":
                        c, q = a
                        wait(pe, "sp", img, ("load_x", c))
                        for j in range(4):
                            ins = pe.transpose(bank[:, j * P:(j + 1) * P],
                                               x_in[:, c % 2, (4 * q + j) * P:(4 * q + j + 1) * P], ident[:, :])
                        finish(ins, "pe", s)
                    elif kind == "embed":
                        c = a[0]
                        wait(pe, "dve", img, ("x_turn", c, 1))
                        r = c % 2
                        finish(three(bank[:, 0:D], [((xt_hi[:, r, k, :], xt_lo[:, r, k, :]), (we_hi[:, k, :], we_lo[:, k, :]))
                                                    for k in range(KT)]), "pe", s)
                    elif kind == "xn_turn":
                        c = a[0]
                        r = CH[c]
                        wait(pe, "dve", img, ("ln1_apply", c))
                        settle(pe)
                        for hf in range(DT):
                            ins = pe.transpose(bank[:, hf * r:(hf + 1) * r], xn[0:r, c, hf * P:(hf + 1) * P],
                                               ident[0:r, 0:r])
                        finish(ins, "pe", s)
                    elif kind in ("decay_proj", "q_proj", "k_proj", "gate_proj"):
                        hf, n = a
                        if kind == "decay_proj":
                            wait(pe, "dve", img, ("xn_turn", 4), 1)
                        w = {"decay_proj": 0, "q_proj": 1, "k_proj": 2, "gate_proj": 3}[kind]
                        o, t = slice(hf * P, (hf + 1) * P), slice(n * NW, (n + 1) * NW)
                        finish(three(bank[:, 0:NW], [((w5[:, w, 0, k, o], w5[:, w, 1, k, o]),
                                                      (xn_hi[:, k, t], xn_lo[:, k, t])) for k in range(DT)]), "pe", s)
                    elif kind == "v_proj":
                        c = a[0]
                        t = slice(ST[c], ST[c] + P)
                        finish(three(bank[:, 0:D], [((xn_hi[:, k, t], xn_lo[:, k, t]),
                                                     (w5[:, 4, 0, k, :], w5[:, 4, 1, k, :])) for k in range(DT)]), "pe", s)
                    elif kind == "scores":
                        c = a[0]
                        r = CH[c]
                        if c == 0:
                            wait(pe, "dve", img, ("qk_split", 1))
                            wait(pe, "pool", img, ("qk_split", 1))
                        for hf in range(DT):
                            for n, (kk, qq) in enumerate(((k_hi, q_hi), (k_hi, q_lo), (k_lo, q_hi))):
                                for j in range(4):
                                    rows_j = slice(32 * j, 32 * j + 32)
                                    ins = pe.matmul(ps[j][:, hf * 2 * r:(hf + 1) * 2 * r].rearrange("p (e t) -> p e t", e=2),
                                                    kk[rows_j, hf, ST[c]:ST[c] + P], qq[rows_j, hf, :, ST[c]:ST[c] + r],
                                                    start=(n == 0), stop=(n == 2))
                        finish(ins, "pe", s)
                    elif kind == "k_turn":
                        c = a[0]
                        for hf in range(DT):
                            ins = pe.transpose(bank[:, hf * P:(hf + 1) * P], gk[:, hf, ST[c]:ST[c] + P], ident[:, :])
                        finish(ins, "pe", s)
                    elif kind == "state":
                        c = a[0]
                        wait(pe, "act", img, ("k_turn", c))
                        wait(pe, "act", img, ("v_proj", 4))
                        for hf in range(DT):
                            ins = pe.matmul(bank[:, hf * P:(hf + 1) * P].rearrange("p (n e v) -> p n e v", n=4, e=2),
                                            kt[:, c % 2, hf * P:(hf + 1) * P],
                                            vp[:, c, 4 * hf:4 * hf + 4, 0:3:2, :], start=True, stop=True)
                        finish(ins, "pe", s)
                    elif kind == "mix":
                        c = a[0]
                        r = CH[c]
                        wait(pe, "dve", img, ("scores", c))
                        if c:
                            wait(pe, "dve", img, ("state", c - 1))
                        for hf in range(DT):
                            cols = slice(hf * r, (hf + 1) * r)
                            if c:
                                pe.matmul(bank[:, cols], state[:, c % 2, hf, :], zq[:, hf, ST[c]:ST[c] + r],
                                          start=True, stop=False, skip_group_check=True)
                            for e in range(2):
                                for j in range(4):
                                    v48 = vp[0:r, c, 4 * hf + j, :, :].rearrange("p a v -> p (a v)")
                                    ins = pe.matmul(bank[32 * j:32 * j + 32, cols], v48[:, e * HD:e * HD + 2 * HD],
                                                    att[0:r, c % 2, j, 2 * hf + e, 0:r],
                                                    start=(c == 0 and e == 0), stop=(e == 1), skip_group_check=True)
                        finish(ins, "pe", s)
                    elif kind == "head_norm":
                        c = a[0]
                        w = DT * CH[c]
                        wait(pe, "act", img, ("mix", c))
                        finish(pe.matmul(bank[:, 0:w], blocks[:, :, :].rearrange("p n v -> p (n v)"), sq[:, c % 2, 0:w],
                                         start=True, stop=True), "pe", s)
                    elif kind == "attn_out":
                        c = a[0]
                        r = CH[c]
                        wait(pe, "dve", img, ("head_norm", c))
                        for hf in range(DT):
                            ins = pe.matmul(bank[0:r, 0:D], og[:, c % 2, hf, 0:r], wo_sb[:, hf, :],
                                            start=(hf == 0), stop=(hf == 1))
                        finish(ins, "pe", s)
                    elif kind == "xn2_turn":
                        c = a[0]
                        r = CH[c]
                        wait(pe, "dve", img, ("ln2_apply", c))
                        settle(pe)
                        for hf in range(DT):
                            ins = pe.transpose(bank[:, hf * r:(hf + 1) * r], xn2[0:r, c, hf * P:(hf + 1) * P],
                                               ident[0:r, 0:r])
                        finish(ins, "pe", s)
                    elif kind == "router":
                        c = a[0]
                        r = CH[c]
                        wait(pe, "act", img, ("xn2_turn", c))
                        for hf in range(DT):
                            ins = pe.matmul(bank[0:r, 0:E], x2t[:, c % 2, hf, 0:r], wr_sb[:, hf, :],
                                            start=(hf == 0), stop=(hf == 1))
                        finish(ins, "pe", s)
                    elif kind == "rank":
                        wait(pe, "dve", img, ("top2",))
                        for c in range(NC):
                            r = CH[c]
                            pe.matmul(bank[0:r, c * E:(c + 1) * E], strict[0:r, 0:r], work[0:r, 0, c, :],
                                      start=True, stop=False)
                            ins = pe.matmul(bank[0:r, c * E:(c + 1) * E], ones[:, 0:r], cum[:, c, :],
                                            start=False, stop=True)
                        finish(ins, "pe", s)

            images(pe, steps)
            attention_over(pe)
            experts(pe, expert_steps)


WEIGHT_LOADS = 19
CONSTS = 20
ACT_CHAIN = 17
DVE_CHAIN = 100

_INS = ["x", "txt", "L0_tok_weight", "L0_tok_weighted_sum", "L0_attn_Wq", "L0_attn_Wk", "L0_attn_Wv", "L0_attn_Wg1",
        "L0_attn_Wg2", "L0_attn_bg2", "L0_attn_Wg", "L0_attn_g_norm_w", "L0_attn_Wo", "L0_ffn_Wr", "L0_ffn_W1",
        "L0_ffn_W3", "L0_ffn_W2"]


def build(nc, args, out):
    slot_table = nc.dram_tensor("slot_table", (TABLE, 2), F32).ap()
    xn_rows = nc.dram_tensor("xn_rows", (T + SPARE, D), F32).ap()
    fusion_kernel(nc, *args, out, slot_table, xn_rows)


def kernel(**inputs):
    import concourse.bacc as bacc
    from concourse.bass_utils import run_bass_kernel_spmd

    nc = bacc.Bacc("TRN2", target_bir_lowering=False, num_devices=1)
    arrays, args = {}, []
    for name in _INS:
        a = np.ascontiguousarray(inputs[name])
        arrays[f"in_{name}"] = a
        args.append(nc.dram_tensor(f"in_{name}", a.shape, mybir.dt.from_np(a.dtype), kind="ExternalInput").ap())
    out = nc.dram_tensor("out_rows", (T + SPARE, D), F32, kind="ExternalOutput").ap()
    build(nc, args, out)
    result = run_bass_kernel_spmd(nc, [arrays], core_ids=[0]).results[0]["out_rows"]
    return result[:T].reshape(B, L, D)
```

```python
from contextlib import ExitStack

import numpy as np

import concourse.bass as bass
from concourse import mybir

F32 = mybir.dt.float32
F32R = mybir.dt.float32r
I32 = mybir.dt.int32
ALU = mybir.AluOpType
ACT = mybir.ActivationFunctionType
AX = mybir.AxisListType

P = 128
B, S, D, TX = 4, 512, 256, 32
DP = 4
L = S + TX
T = B * L
KD = D * DP
KT = KD // P
DT = D // P
H, HD = 16, 16
CH = [P] * (S // P) + [TX]
NC = len(CH)
ST = [P * c for c in range(NC)]
LP = P * NC
NW = L // 2
EPS = 1e-5
GLN = 16.0
QSCALE = HD ** -0.5
E, FF, TOPK = 8, 1024, 2
CAP = -(-T * TOPK * 5 // (4 * E))
FT = FF // P
TABLE = -(-(E * CAP + TOPK * LP) // P) * P
CLAMP = 10000.0
SPARE = 1 << (CAP - 1).bit_length()

PROLOGUE = [
    ("load_x", 1), ("load_x", 0), ("load_txt",), ("x_turn", 0, 0), ("x_turn", 0, 1), ("load_x", 2),
    ("x_turn", 1, 0), ("load_x", 3), ("x_turn", 1, 1), ("embed", 0), ("ln1_stats", 0), ("ln1_rsqrt", 0),
    ("x_turn", 2, 0), ("x_turn", 2, 1), ("embed", 1), ("ln1_apply", 0), ("ln1_stats", 1), ("ln1_rsqrt", 1),
    ("ln1_rsqrt", 4), ("embed", 2), ("ln1_stats", 4), ("ln1_apply", 4), ("ln1_stats", 2), ("ln1_rsqrt", 2),
    ("x_turn", 3, 0), ("x_turn", 3, 1), ("ln1_apply", 1), ("xn_turn", 0), ("embed", 3), ("ln1_stats", 3),
    ("ln1_apply", 2), ("ln1_apply", 3), ("xn_turn", 1), ("ln1_rsqrt", 3), ("xn_turn", 2), ("xn_turn", 4),
    ("xn_turn", 3), ("hold_residual",), ("decay_proj", 0, 0), ("decay_proj", 1, 0), ("decay_proj", 0, 1),
    ("decay_proj", 1, 1), ("decay_abs", 0), ("v_proj", 0), ("v_proj", 1), ("decay_log", 0), ("decay_log", 1),
    ("v_proj", 2), ("decay_abs", 1), ("v_proj", 4), ("v_proj", 3), ("decay_sum", 0), ("decay_exp", 0),
    ("decay_sum", 1), ("range",), ("range_sum",), ("decay_exp", 1),
]
BODY = [
    ("k_proj", 0, 0), ("load_x", 1), ("k_proj", 0, 1), ("q_proj", 0, 0), ("q_proj", 0, 1), ("qk_split", 0),
    ("q_proj", 1, 1), ("load_txt",), ("k_proj", 1, 0), ("q_proj", 1, 0), ("load_x", 0), ("x_turn", 0, 0),
    ("k_proj", 1, 1), ("qk_split", 1), ("gate_proj", 0, 0), ("load_x", 2), ("x_turn", 0, 1), ("gate_proj", 0, 1),
    ("gate_proj", 1, 0), ("gate_proj", 1, 1), ("x_turn", 1, 0), ("embed", 0), ("x_turn", 1, 1), ("load_x", 3),
    ("ln1_stats", 0), ("exact",), ("ln1_stats", 4), ("x_turn", 2, 0), ("ln1_rsqrt", 4), ("scores", 0),
    ("ln1_apply", 4), ("ln1_stats", 1), ("top2", 0), ("k_turn", 0), ("embed", 1), ("x_turn", 2, 1), ("scores", 1),
    ("state", 0), ("ln1_rsqrt", 0), ("mix", 0), ("x_turn", 3, 0), ("embed", 2), ("top2", 1), ("k_turn", 1),
    ("ln1_apply", 0), ("scores", 2), ("state", 1), ("ln1_rsqrt", 1), ("head_norm", 0), ("x_turn", 3, 1),
    ("mix", 1), ("k_turn", 2), ("xn_turn", 0), ("ln1_stats", 2), ("ln1_apply", 1), ("gate_exp",), ("ln1_rsqrt", 2),
    ("slots", 0), ("embed", 3), ("attn_out", 0), ("ln2_stats", 0), ("rank",), ("scores", 3), ("state", 2),
    ("head_norm", 1), ("mix", 2), ("k_turn", 3), ("attn_out", 1), ("xn_turn", 4), ("ln1_apply", 2),
    ("ln1_stats", 3), ("ln1_rsqrt", 3), ("xn_turn", 1), ("ln2_stats", 1), ("ln2_apply", 0), ("ln2_rsqrt", 0),
    ("scores", 4), ("slots", 1), ("ln1_apply", 3), ("xn2_turn", 0), ("state", 3), ("ln2_rsqrt", 1),
    ("table_scatter",), ("head_norm", 2), ("mix", 3), ("xn_turn", 2), ("attn_out", 2), ("mix", 4), ("router", 0),
    ("ln2_apply", 1), ("xn_turn", 3), ("v_proj", 0), ("ln2_stats", 2), ("head_norm", 3), ("ln2_rsqrt", 2),
    ("xn2_turn", 1), ("v_proj", 1), ("attn_out", 3), ("ln2_stats", 3), ("head_norm", 4), ("router", 1),
    ("ln2_apply", 2), ("decay_proj", 1, 0), ("decay_proj", 0, 0), ("decay_proj", 0, 1), ("decay_proj", 1, 1),
    ("decay_abs", 0), ("decay_abs", 1), ("attn_out", 4), ("decay_log", 0), ("v_proj", 2), ("ln2_rsqrt", 3),
    ("decay_log", 1), ("decay_sum", 0), ("xn2_turn", 2), ("ln2_stats", 4), ("ln2_apply", 3), ("v_proj", 3),
    ("ln2_rsqrt", 4), ("decay_exp", 0), ("router", 2), ("xn2_turn", 3), ("decay_exp", 1), ("v_proj", 4),
    ("decay_sum", 1), ("ln2_apply", 4), ("range",), ("router", 3), ("xn2_turn", 4), ("router", 4),
    ("hold_residual",), ("range_sum",),
]
FOR_NEXT = {"load_x", "load_txt", "x_turn", "embed", "ln1_stats", "ln1_rsqrt", "ln1_apply", "xn_turn",
            "hold_residual", "decay_proj", "decay_abs", "decay_log", "decay_sum", "decay_exp", "v_proj",
            "range", "range_sum"}
FOR_LAST = {"top2", "gate_exp", "rank", "slots", "table_scatter"}
LAST = [s for s in BODY if s[0] not in FOR_NEXT]
ROUTE = [s for s in BODY if s[0] in FOR_LAST]

HALF = FT // 2
W2_AT = {0: [1, 2], 1: [3], 2: [4], 3: [5], 4: [6], 5: [7]}


class Cut:

    def __init__(self, widths):
        self.halves = [(0, widths[0]), (widths[0], widths[1])]
        self.tiles = [(at + r, min(P, width - r)) for at, width in self.halves for r in range(0, width, P)]
        self.half_of = [h for h, (_, width) in enumerate(self.halves) for r in range(0, width, P)]
        self.last = [max(n for n, h in enumerate(self.half_of) if h == half) for half in range(2)]
        self.slots = sum(widths)
        self.body = self.expert_body()
        self.ahead = [("load_w13", 0)] + [("w13_split", f) for f in range(HALF)] + [("load_w13", 1)] + \
                     [("w13_split", f) for f in range(HALF, FT)]
        self.first = [("load_gather_index",)] + [("gather", n) for n in range(len(self.tiles))] + \
                     [("xe_turn", n) for n in range(len(self.tiles))]
        self.last_body = [s for s in self.body if s[0] not in NEXT_EXPERT]

    def expert_body(self):
        steps = [("load_w2", 0), ("load_w2", 1), ("load_w13", 0), ("load_w13", 1), ("load_gather_index",),
                 ("load_scatter_index",), ("w2_split", 0)]
        for f in range(FT):
            steps += [("up", f, 0)]
            if f:
                steps += [("h_split", f - 1, 1)]
                if f < FT - 1:
                    steps += [("w13_split", f - 1)]
            if f in W2_AT:
                steps += [("w2_split", w) for w in W2_AT[f]]
            if 1 <= f < 1 + len(self.tiles):
                steps += [("gather", f - 1)]
            steps += [("up", f, 1), ("h_split", f, 0)]
        steps += [("h_split", FT - 1, 1), ("w13_split", FT - 2), ("w13_split", FT - 1)]
        for n in range(len(self.tiles)):
            steps += [("down", n), ("scatter", n), ("xe_turn", n)]
        return steps + [("scattered",)]


NEXT_EXPERT = {"load_w13", "w13_split", "load_gather_index", "gather", "xe_turn"}
WHOLE = Cut((CAP // 2, CAP - CAP // 2))
SHORT = Cut((CAP // 2, 2 * P))
EXPERT, EXPERT_AHEAD, NT = WHOLE.body, WHOLE.ahead, len(WHOLE.tiles)
_at = LAST.index(("scores", 0))
LAST = LAST[:_at] + [EXPERT_AHEAD[0]] + LAST[_at:]
for _i, _s in enumerate(EXPERT_AHEAD[1:]):
    _at = LAST.index(("scores", 1)) + 6 + 5 * _i
    LAST.insert(_at, _s)

PROJ = ["decay_proj", "v_proj", "gate_proj", "q_proj", "k_proj"]
_n = 0
BANK = {}
for _s in BODY:
    if _s[0] in PROJ:
        BANK[_s] = _n % 4
        _n += 1
for _c in range(NC):
    BANK["mix", _c] = 4
    BANK["k_turn", _c] = 5
    BANK["state", _c] = 7
    BANK["head_norm", _c] = 5
    BANK["attn_out", _c] = 7
    BANK["xn2_turn", _c] = 5
    BANK["router", _c] = 7
    BANK["embed", _c] = (7, 5)[_c % 2]
    BANK["xn_turn", _c] = (5, 7)[_c % 2]
    for _q in range(2):
        BANK["x_turn", _c, _q] = 6
BANK["rank",] = 5
BANK["range_sum",] = 6
for _t in range(NT):
    BANK["down", _t] = 4 + _t % 2
    BANK["xe_turn", _t] = 6 + _t % 2
READER = {
    "x_turn": "dve", "embed": "act", "xn_turn": "dve", "decay_proj": "act", "v_proj": "act",
    "gate_proj": "act", "q_proj": "dve", "k_proj": "dve", "scores": "dve", "k_turn": "act",
    "state": "dve", "mix": "dve", "head_norm": "act", "attn_out": "dve", "xn2_turn": "act",
    "router": "dve", "rank": "dve", "range_sum": "dve", "exact": "dve", "up": "dve", "down": "dve", "xe_turn": "dve",
}
PARTS = {
    "load_x": {"sp": 16}, "load_txt": {"sp": 16}, "hold_residual": {"pool": 1},
    "x_turn": {"pe": 1, "act": 1, "dve": 1}, "embed": {"pe": 1, "act": 1},
    "ln1_stats": {"dve": 1}, "ln1_rsqrt": {"act": 1}, "ln1_apply": {"dve": 1},
    "xn_turn": {"pe": 1, "act": 1, "dve": 1},
    "decay_proj": {"pe": 1, "act": 1}, "decay_abs": {"dve": 1}, "decay_log": {"act": 1},
    "decay_sum": {"dve": 1}, "decay_exp": {"act": 1}, "v_proj": {"pe": 1, "act": 1},
    "gate_proj": {"pe": 1, "act": 1}, "q_proj": {"pe": 1, "dve": 1}, "k_proj": {"pe": 1, "dve": 1},
    "qk_split": {"act": 1, "dve": 1, "pool": 1}, "range": {"dve": 1}, "range_sum": {"pe": 1, "dve": 1},
    "exact": {"dve": 1},
    "scores": {"pe": 1, "dve": 1}, "k_turn": {"pe": 1, "act": 1}, "state": {"pe": 1, "dve": 1},
    "mix": {"pe": 1, "act": 1, "dve": 1}, "head_norm": {"pe": 1, "act": 1, "dve": 1},
    "attn_out": {"pe": 1, "dve": 1, "sp": 16},
    "ln2_stats": {"dve": 1}, "ln2_rsqrt": {"act": 1}, "ln2_apply": {"dve": 1, "sp": 16},
    "xn2_turn": {"pe": 1, "act": 1}, "router": {"pe": 1, "dve": 1},
    "top2": {"dve": 1}, "gate_exp": {"act": 1}, "rank": {"pe": 1}, "slots": {"dve": 1},
    "table_scatter": {"pool": 1},
    "load_w13": {"sp": 16}, "load_w2": {"sp": 16}, "load_gather_index": {"sp": 16},
    "load_scatter_index": {"sp": 16}, "gather": {"pool": 16},
    "w13_split": {"act": 1, "pool": 1}, "w2_split": {"act": 1, "pool": 1},
    "xe_turn": {"pe": 1, "act": 1, "dve": 1}, "up": {"pe": 1, "act": 1, "dve": 1},
    "h_split": {"act": 1, "dve": 1}, "down": {"pe": 1, "dve": 1}, "scatter": {}, "scattered": {"pool": 1},
}


TRANSFERS = {"load_w13": 2, "load_gather_index": 4, "load_scatter_index": 4}


def count_of(steps, kind):
    return sum(s[0] == kind for s in steps)


class Walk:

    def __init__(self, steps, i, prologue, body, cut=None):
        self.steps, self.i, self.prologue, self.body, self.cut = steps, i, prologue, body, cut
        self.waited = {}

    def banks(self, step):
        if step[0] in ("scores", "exact"):
            return range(4)
        if step[0] == "x_turn" and self.i is None:
            return [(2 * step[1] + step[2]) % 4]
        if step[0] == "up":
            return [2 * step[2], 2 * step[2] + 1]
        return [BANK[step]] if step in BANK else []

    def times(self, step, back=0):
        of_kind = [s for s in (self.prologue if self.i is None else self.body) if s[0] == step[0]]
        index = of_kind.index(step) + 1
        if self.i is None:
            return None if back else index
        per, before = count_of(self.body, step[0]), count_of(self.prologue, step[0])
        return (self.i - back) * per + (before or count_of(BODY + EXPERT, step[0])) + index

    def before_in_bank(self, step, bank):
        own = self.steps if step in self.steps else self.prologue
        for other in reversed(own[:own.index(step)]):
            if bank in self.banks(other):
                return other, 0
        if self.i is None:
            return None, 0
        for other in reversed(self.body):
            if bank in self.banks(other):
                return other, 1
        return None, 0


def image(steps, b):
    return Walk(steps, b, PROLOGUE, BODY)


def expert(cut, steps, e):
    return Walk(steps, e, cut.ahead + cut.first, cut.body, cut)


def fusion_kernel(nc, x, txt, tok_weight, tok_sum, wq, wk, wv, wg1, wg2, bg2, wg, g_norm, wo, wr, w1, w3, w2, out,
                  slot_table, xn_rows):
    ctx = ExitStack()
    with ctx:
        def sb(name, shape, dt=F32):
            return ctx.enter_context(nc.sbuf_tensor("sb_" + name, shape, dt))

        def sem(name):
            return ctx.enter_context(nc.semaphore(name))

        def psum(name):
            return ctx.enter_context(nc.psum_tensor(name, [P, 512], F32))

        RA = 4 * KT * P + 2 * KT * D + 10 * DT * D
        rarena = sb("rounded", [P, RA + 2 * FT * CAP + 2 * DT * CAP], F32R)
        at = [0]

        def rc(*shape):
            n = int(np.prod(shape))
            v = rarena[:, at[0]:at[0] + n]
            at[0] += n
            names = "abcdef"[:len(shape)]
            if len(shape) == 1:
                return v
            return v.rearrange(f"p ({' '.join(names)}) -> p {' '.join(names)}", **dict(zip(names, shape)))

        xt_hi, xt_lo = rc(2, KT, P), rc(2, KT, P)
        we_hi, we_lo = rc(KT, D), rc(KT, D)
        w5 = rc(5, 2, DT, D)
        xn_hi, xn_lo = rc(DT, LP), rc(DT, LP)
        q_hi, q_lo = rc(DT, 2, LP), rc(DT, 2, LP)
        k_hi, k_lo = rc(DT, LP), rc(DT, LP)

        at[0] = 0
        w13 = rc(FT, 2, 2, DT, P)
        w2s = rc(FT, 2, D)
        at[0] = 2 * 2 * KT * P + 2 * KT * D + 5 * 2 * DT * D
        h_hi, h_lo = rc(FT, CAP), rc(FT, CAP)
        xe_hi, xe_lo = rc(DT, CAP), rc(DT, CAP)
        x_in = sb("x_in", [P, 2, KD])
        h_new = sb("h_new", [P, NC, D])
        h_res = sb("h_res", [P, NC, D])
        xn = sb("xn", [P, NC, D])
        zq = sb("zq", [P, DT, L])
        gk = sb("gk", [P, DT, L])
        dec = sb("dec", [P, DT, L])
        gate = sb("gate", [P, DT, L])
        vp = sb("vp", [P, NC, 8, 3, HD])
        att = sb("att", [P, 2, 4, 4, P])
        kt = sb("kt", [P, 2, D])
        state = sb("state", [P, 2, DT, P])
        state0 = sb("state0", [P, DT, P])
        lowest = sb("lowest", [P, 2])
        floor = sb("floor", [P, 1])
        exact_f = sb("exact_f", [1, 2])
        exact_i = sb("exact_i", [1, 1], I32)
        overfull_f = sb("overfull_f", [1, 1])
        overfull_i = sb("overfull_i", [1, 1], I32)
        stmp = sb("stmp", [P, DT, P])
        sq = sb("sq", [P, 2, DT * P])
        rs = sb("rs", [P, DT * P])
        og = sb("og", [P, 2, DT, P])
        xn2 = sb("xn2", [P, NC, D])
        x2t = sb("x2t", [P, 2, DT, P])
        raw13 = sb("raw13", [P, 2048])
        raw2 = sb("raw2", [P, 1024])
        wo_sb = sb("wo", [P, DT, D])
        wr_sb = sb("wr", [P, DT, E])
        ident = sb("ident", [P, P])
        upper = sb("upper", [P, P])
        strict = sb("strict", [P, P])
        ones = sb("ones", [P, P])
        blocks = sb("blocks", [P, 8, HD])
        evenodd = sb("evenodd", [P, 2])
        tokw = sb("tokw", [P, DT, DP])
        bias = sb("bias", [P, DT])
        gnw = sb("gnw", [P, 1])
        eps = sb("eps", [P, 1])
        bn = sb("bn", [P, 2, 6])
        mv = sb("mv", [P, 2, NC, 2])
        ve = sb("ve", [P, 2, NC])
        y0 = sb("y0", [P, 2, NC])
        y1 = sb("y1", [P, 2, 4])
        lg = sb("lg", [P, NC, E])
        pick = sb("pick", [P, 2, NC, E])
        work = sb("work", [P, 2, NC, E])
        tops = sb("tops", [P, 4, NC])
        cum = sb("cum", [P, NC + 1, E])
        expert_no = sb("expert_no", [P, E])
        falling = sb("falling", [P, E])
        valid_rows = sb("valid_rows", [P, 2, NC])
        valid = sb("valid", [P, 2, NC])
        dump = sb("dump", [P, 2, NC])
        posk = sb("posk", [P, 4, 2, NC])
        token_no = sb("token_no", [P, NC])
        slot_of = sb("slot_of", [P, 2, NC], I32)
        rows = sb("rows", [P, 2, NC, 2])
        dummy = sb("dummy", [P, 1])
        tinit = sb("tinit", [P, TABLE // P, 2])
        tinit_i = sb("tinit_i", [P, TABLE // P], I32)

        att_flat = att[:, :, :, :, :].rearrange("p r j n t -> p (r j n t)")
        xe = att_flat[:, 0:NT * D].rearrange("p (n d) -> p n d", n=NT)
        ye = att_flat[:, NT * D:2 * NT * D].rearrange("p (n d) -> p n d", n=NT)
        gate_flat = gate[:, :, :].rearrange("p h t -> p (h t)")
        dec_flat = dec[:, :, :].rearrange("p h t -> p (h t)")
        raw13_half = [raw13[:, :], x_in[:, :, :].rearrange("p r k -> p (r k)")]
        raw2_half = [raw2[:, :], h_new[:, 0:4, :].rearrange("p c d -> p (c d)")]
        g_index = sb("g_index", [P, NT, 2])
        s_index = sb("s_index", [P, NT, 2])
        prod = att[:, :, :, :, :].rearrange("p r j n t -> p (r j n t)")[:, 0:DT * KD].rearrange("p (h k) -> p h k", h=DT)

        ps = [psum(f"ps{i}") for i in range(8)]

        ex_q, ex_a = att_flat[:, 0:2 * L], att_flat[:, 2 * L:4 * L]
        ex_u, ex_s, ex_w = (att_flat[:, i * L:(i + 1) * L] for i in range(4, 7))
        ex_k = raw13[:, 0:2 * L]
        ex_v = xn2[:, :, :].rearrange("p c d -> p (c d)")[:, 0:2 * L]
        ex_o = zq[:, :, :].rearrange("p h t -> p (h t)")
        sel_in = raw2[:, 0:P].rearrange("p (n v) -> p n v", v=HD)
        sel_out = raw2[:, P:2 * P].rearrange("p (n v) -> p n v", v=HD)
        onehot = raw2[:, 2 * P:2 * P + HD]
        hot = raw2[:, 2 * P + HD:2 * P + 3 * HD - 1]

        done = {(e, k): sem(f"{e}_{k}") for k, parts in PARTS.items() for e in parts
                if e != "sp" and k != "gather"}
        moved = {s: sem("_".join(map(str, s))) for s in BODY + EXPERT if "sp" in PARTS[s[0]] or s[0] == "gather"}
        ready = {n: sem(n) for n in (
            "weights_in", "consts_made", "product_made", "we_turned", "we_hi_made", "we_lo_made",
            "split_hi_made", "split_lo_made", "g1_turned", "g1_copied", "decay_w_made",
            "table_out", "table_rows_out", "rows_added", "zero_rows_out", "pads_zeroed", "settled", "exact_none", "embed_weights_in",
            "counts_summed", "most_found", "cut_known")}
        chain = {e: sem(f"{e}_chain") for e in ("act", "dve", "pool")}
        exact = {e: sem(f"exact_{e}") for e in ("pe", "act", "dve")}

        def wait(eng, who, img, step, back=0):
            if img.i is None and step not in img.prologue:
                return
            late = img.prologue if img.i is None else img.body
            mark = late.index(step) - back * len(late)
            key = (who, step if step in moved and who in ("sp", "pool") else step[0])
            if img.waited.get(key, -2 * len(late)) >= mark:
                return
            img.waited[key] = mark
            if step in moved and who in ("sp", "pool"):
                unit = 16 * TRANSFERS.get(step[0], 1)
                if img.i is not None:
                    eng.wait_ge(moved[step], (img.i - back + 2) * unit)
                elif not back:
                    eng.wait_ge(moved[step], unit)
                return
            n = img.times(step, back)
            if n is not None:
                eng.wait_ge(done[who, step[0]], n * PARTS[step[0]][who])

        def finish(ins, who, step):
            if step in moved and who in ("sp", "pool"):
                ins.then_inc(moved[step], 16)
            else:
                ins.then_inc(done[who, step[0]], PARTS[step[0]][who])

        class Chain:

            def __init__(self, who, eng):
                self.who, self.eng, self.base, self.n = who, eng, 0, 0

            def __call__(self, ins):
                self.n += 1
                ins.then_inc(chain[self.who], 1)
                self.eng.wait_ge(chain[self.who], self.base + self.n)

            def start(self, base):
                self.base, self.n = base, 0

        def settle(eng):
            eng.sem_inc(ready["settled"], 1)

        def first_wait_credit(eng, who):
            if who == "sp":
                for step, s in moved.items():
                    if step not in PROLOGUE + WHOLE.ahead + WHOLE.first:
                        eng.sem_inc(s, 16 * TRANSFERS.get(step[0], 1))
            for (e, k), s in done.items():
                if e == who and not count_of(PROLOGUE + WHOLE.ahead + WHOLE.first, k):
                    eng.sem_inc(s, count_of(BODY + EXPERT, k))
            if who in exact:
                eng.sem_inc(exact[who], {"pe": EXACT_PE, "act": EXACT_ACT, "dve": EXACT_DVE}[who])

        def images(eng, walk, chained=None, per=0):
            walk(image(PROLOGUE, None))
            start = chained.base + chained.n if chained else 0
            with eng.Fori(0, B - 1) as b:
                if chained:
                    chained.start(b * per + start)
                walk(image(BODY, b))
                if chained:
                    assert chained.n == per, (chained.who, chained.n)
            if chained:
                chained.start((B - 1) * per + start)
            walk(image(LAST, B - 1))
            walk(image(ROUTE, B))

        def back_first(used, late):
            return used[1], -late.index(used[0])

        def bank_free(pe, img, step):
            late = img.prologue if img.i is None else img.body
            used = {img.before_in_bank(step, bank) for bank in img.banks(step)} - {(None, 0)}
            for other, back in sorted(used, key=lambda u: back_first(u, late)):
                if other == ("rank",):
                    wait(pe, "dve", img, ("slots", 0), back)
                else:
                    wait(pe, READER[other[0]], img, other, back)

        def short_or_whole(eng):
            eng.wait_ge(ready["cut_known"], 1)
            return eng.value_load(overfull_i[0:1, 0:1], min_val=0, max_val=1)

        def experts(eng, walk, overfull, at_end=None):
            for cut, chosen in ((SHORT, overfull == 0), (WHOLE, overfull != 0)):
                with eng.If(chosen):
                    walk(expert(cut, cut.first, None))
                    with eng.Fori(0, E - 1) as e:
                        walk(expert(cut, cut.body, e))
                    walk(expert(cut, cut.last_body, E - 1))
                    if at_end:
                        at_end(cut)

        def attention_over(eng):
            route = image(ROUTE, B)
            wait(eng, "pe", route, ("rank",))
            wait(eng, "dve", route, ("slots", 1))

        def exact_path(eng, img, walk):
            wait(eng, "dve", img, ("range_sum",), 1)
            settle(eng)
            place = eng.value_load(exact_i[0:1, 0:1], min_val=0, max_val=B)
            with eng.If(place != 0):
                walk(place)

        block = ctx.enter_context(nc.Block())

        x_tiles = x.rearrange("b (c p) i d -> (b c) p (i d)", p=P)
        out_rows = out
        CHN = S // P

        @block.sync
        def _(sp):
            first_wait_credit(sp, "sp")

            w13_in = [w.rearrange("e (k p) f -> e p k f", p=P) for w in (w1, w3)]
            w2_in = w2.rearrange("e (f p) d -> e p f d", p=P)
            table = slot_table
            ahead = expert(WHOLE, WHOLE.ahead, None)

            def expert_step(ex, s):
                kind, a = s[0], s[1:]
                this = 0 if ex.i is None else ex.i
                nxt = 0 if ex.i is None else ex.i + 1
                if kind == "load_w13":
                    prev = ("w13_split", FT - 1 if a[0] else HALF - 1)
                    wait(sp, "act", ex, prev, 1)
                    wait(sp, "pool", ex, prev, 1)
                    if ex.i is None:
                        wait(sp, "dve", image(LAST, B - 1), ("exact",))
                        wait(sp, "pe", image(BODY, B - 2), ("x_turn", 3, 1))
                    raw = raw13_half[a[0]].rearrange("p (w k f) -> p w k f", w=2, k=DT)
                    cols = slice(a[0] * HALF * P, (a[0] + 1) * HALF * P)
                    for w in range(2):
                        sp.dma_start(raw[:, w, :, :], w13_in[w][nxt, :, :, cols]).then_inc(moved[s], 16)
                elif kind == "load_w2":
                    prev = ("w2_split", FT - 1 if a[0] else HALF - 1)
                    wait(sp, "act", ex, prev, 1)
                    wait(sp, "pool", ex, prev, 1)
                    finish(sp.dma_start(raw2_half[a[0]].rearrange("p (f d) -> p f d", f=HALF),
                                        w2_in[this, :, a[0] * HALF:(a[0] + 1) * HALF, :]), "sp", s)
                elif kind in ("load_gather_index", "load_scatter_index"):
                    gathers = kind == "load_gather_index"
                    if gathers:
                        for n in range(len(ex.cut.tiles)):
                            wait(sp, "pool", ex, ("gather", n), 1)
                    else:
                        wait(sp, "pool", ex, ("scattered",), 1)
                        wait(sp, "dve", ex, ("down", len(ex.cut.tiles) - 1), 1)
                    dst = g_index if gathers else s_index
                    base = (nxt if gathers else this) * CAP
                    for h, last in enumerate(ex.cut.last):
                        first = ex.cut.half_of.index(h)
                        at, n = ex.cut.halves[h][0], last - first
                        sp.dma_start(dst[:, first:last, :],
                                     table[bass.ds(base + at, n * P), :].rearrange("(n p) t -> p n t", p=P)
                                     ).then_inc(moved[s], 16)
                        at, r = ex.cut.tiles[last]
                        sp.dma_start(dst[0:r, last, :], table[bass.ds(base + at, r), :]).then_inc(moved[s], 16)

            def expert_steps(ex):
                for s in ex.steps:
                    if "sp" in PARTS[s[0]]:
                        expert_step(ex, s)

            def steps(img):
                nxt = 0 if img.i is None else img.i + 1
                for s in img.steps:
                    kind, a = s[0], s[1:]
                    if kind in NEXT_EXPERT:
                        expert_step(ahead, s)
                        continue
                    if kind == "load_x":
                        c = a[0]
                        prev = ("x_turn", c - 2, 1) if c >= 2 else ("x_turn", c + 2, 1)
                        wait(sp, "pe", img, prev, 0 if c >= 2 else 1)
                        finish(sp.dma_start(x_in[:, c % 2, :], x_tiles[nxt * CHN + c, :, :]), "sp", s)
                    elif kind == "load_txt":
                        if img.i is None:
                            sp.wait_ge(ready["pads_zeroed"], 1)
                        else:
                            wait(sp, "pool", img, ("hold_residual",), 1)
                        finish(sp.dma_start(h_new[0:TX, NC - 1, :], txt[nxt, :, :]), "sp", s)
                    elif kind == "attn_out":
                        c = a[0]
                        wait(sp, "dve", img, s)
                        finish(sp.dma_start(out_rows[bass.ds(img.i * L + ST[c], CH[c]), :],
                                     h_res[0:CH[c], c, :]), "sp", s)
                    elif kind == "ln2_apply":
                        c = a[0]
                        wait(sp, "dve", img, s)
                        finish(sp.dma_start(xn_rows[bass.ds(img.i * L + ST[c], CH[c]), :],
                                     xn2[0:CH[c], c, :]), "sp", s)

            sp.dma_start(xn[:, 0:DT, :], tok_sum.rearrange("(h p) i -> p h i", p=P)).then_inc(ready["embed_weights_in"], 16)
            sp.dma_start(tokw[:, :, :], tok_weight.rearrange("(h p) d -> p h d", p=P)).then_inc(ready["embed_weights_in"], 16)
            images(sp, steps)
            attention_over(sp)
            overfull = short_or_whole(sp)
            wait(sp, "pool", image(ROUTE, B), ("table_scatter",))
            experts(sp, expert_steps, overfull,
                    lambda cut: sp.wait_ge(ready["rows_added"], 16 * len(cut.tiles) * E))
            sp.wait_ge(ready["zero_rows_out"], 32)

        @block.gpsimd
        def _(pool):
            made = ready["consts_made"]
            first_wait_credit(pool, "pool")
            link = Chain("pool", pool)
            pool.memset(h_new[:, NC - 1, :], 0.0).then_inc(ready["pads_zeroed"], 1)
            link(pool.memset(ident[:, :], 0.0))
            pool.affine_select(out=ident[:, :], in_=ident[:, :], compare_op=ALU.not_equal, fill=1.0, base=0,
                               pattern=[[-1, P]], channel_multiplier=1).then_inc(made, 1)
            link(pool.memset(ones[:, :], 1.0))
            pool.affine_select(out=upper[:, :], in_=ones[:, :], compare_op=ALU.is_ge, fill=0.0, base=0,
                               pattern=[[1, P]], channel_multiplier=-1).then_inc(made, 1)
            pool.affine_select(out=strict[:, :], in_=ones[:, :], compare_op=ALU.is_gt, fill=0.0, base=0,
                               pattern=[[1, P]], channel_multiplier=-1).then_inc(made, 1)
            ones3 = ones[:, :].rearrange("p (n v) -> p n v", v=HD)
            link(pool.affine_select(out=blocks[:, :, :], in_=ones3, compare_op=ALU.is_ge, fill=0.0, base=0,
                                    pattern=[[-HD, P // HD], [0, HD]], channel_multiplier=1))
            pool.affine_select(out=blocks[:, :, :], in_=blocks[:, :, :], compare_op=ALU.is_ge, fill=0.0,
                               base=HD - 1, pattern=[[HD, P // HD], [0, HD]], channel_multiplier=-1).then_inc(made, 1)
            pool.memset(eps[:, :], EPS).then_inc(made, 1)
            pool.memset(kt[:, :, :], 0.0).then_inc(made, 1)
            pool.memset(vp[:, :, :, :, :], 0.0).then_inc(made, 1)
            pool.memset(lg[:, :, :], 0.0).then_inc(made, 1)
            pool.memset(cum[:, :, :], 0.0).then_inc(made, 1)
            pool.iota(expert_no[:, :], [[1, E]], base=0, channel_multiplier=0,
                      allow_small_or_imprecise_dtypes=True).then_inc(made, 1)
            pool.iota(falling[:, :], [[-1, E]], base=E, channel_multiplier=0,
                      allow_small_or_imprecise_dtypes=True).then_inc(made, 1)
            pool.iota(dump[:, :, :], [[LP, 2], [P, NC]], base=E * CAP, channel_multiplier=1,
                      allow_small_or_imprecise_dtypes=True).then_inc(made, 1)
            pool.iota(token_no[:, :], [[P, NC]], base=-2 * L, channel_multiplier=1,
                      allow_small_or_imprecise_dtypes=True).then_inc(made, 1)
            pool.iota(tinit_i[:, :], [[1, TABLE // P]], base=0, channel_multiplier=TABLE // P).then_inc(made, 1)
            pool.memset(valid[:, :, :], 0.0).then_inc(made, 1)
            link(pool.memset(valid_rows[:, :, :], 1.0))
            pool.affine_select(out=valid_rows[:, :, :], in_=valid_rows[:, :, :], compare_op=ALU.is_gt, fill=0.0,
                               base=TX + (NC - 1) * P, pattern=[[0, 2], [-P, NC]], channel_multiplier=-1).then_inc(made, 1)
            pool.memset(xn_hi[:, :, L:LP].bitcast(F32), 0.0).then_inc(made, 1)
            pool.memset(xn_lo[:, :, L:LP].bitcast(F32), 0.0).then_inc(made, 1)
            pool.memset(k_hi[:, :, L:LP].bitcast(F32), 0.0).then_inc(made, 1)
            pool.memset(k_lo[:, :, L:LP].bitcast(F32), 0.0).then_inc(made, 1)
            pool.memset(tinit[:, :, 1:2], 0.0).then_inc(made, 1)

            ahead = expert(WHOLE, WHOLE.ahead, None)

            def expert_step(ex, s):
                kind, a = s[0], s[1:]
                if kind == "w13_split":
                    f = a[0]
                    wait(pool, "act", ex, s)
                    raw = raw13_half[f // HALF].rearrange("p (w k f) -> p w k f", w=2, k=DT)
                    cols = slice(f % HALF * P, (f % HALF + 1) * P)
                    for w in range(2):
                        ins = pool.tensor_tensor(w13[:, f, w, 1, :, :], raw[:, w, :, cols],
                                                 w13[:, f, w, 0, :, :].bitcast(F32), ALU.subtract)
                    finish(ins, "pool", s)
                elif kind == "w2_split":
                    f = a[0]
                    wait(pool, "act", ex, s)
                    finish(pool.tensor_tensor(w2s[:, f, 1, :], raw2_half[f // HALF][:, f % HALF * D:(f % HALF + 1) * D],
                                              w2s[:, f, 0, :].bitcast(F32), ALU.subtract), "pool", s)
                elif kind == "gather":
                    n = a[0]
                    wait(pool, "sp", ex, ("load_gather_index",))
                    wait(pool, "pe", ex, ("xe_turn", n), 1)
                    r = ex.cut.tiles[n][1]
                    settle(pool)
                    finish(pool.indirect_dma_start(
                        xe[0:r, n, :], None, xn_rows,
                        bass.IndirectOffsetOnAxis(ap=g_index[0:r, n, 0:1].bitcast(I32), axis=0)), "pool", s)
                elif kind == "scatter":
                    n = a[0]
                    wait(pool, "dve", ex, ("down", n))
                    r = ex.cut.tiles[n][1]
                    settle(pool)
                    pool.indirect_dma_start(
                        out_rows, bass.IndirectOffsetOnAxis(ap=s_index[0:r, n, 0:1].bitcast(I32), axis=0),
                        ye[0:r, n, :], None, compute_op=ALU.add).then_inc(ready["rows_added"], 16)
                elif kind == "scattered":
                    pool.wait_ge(ready["rows_added"], (ex.i + 1) * (16 * len(ex.cut.tiles)))
                    pool.sem_inc(done["pool", "scattered"], 1)

            def expert_steps(ex):
                for s in ex.steps:
                    if "pool" in PARTS[s[0]] or s[0] == "scatter":
                        expert_step(ex, s)

            def steps(img):
                for s in img.steps:
                    kind, a = s[0], s[1:]
                    if kind in NEXT_EXPERT:
                        expert_step(ahead, s)
                        continue
                    if kind == "hold_residual":
                        wait(pool, "dve", img, ("ln1_apply", 3))
                        wait(pool, "act", img, ("embed", 3))
                        for c in range(NC):
                            wait(pool, "sp", img, ("attn_out", c))
                        wait(pool, "dve", img, ("attn_out", 4))
                        wait(pool, "dve", img, ("ln2_apply", 4))
                        wait(pool, "dve", img, ("state", 0))
                        wait(pool, "pe", img, ("mix", 0))
                        settle(pool)
                        pool.memset(state0[:, :, :], 0.0)
                        finish(pool.tensor_copy(h_res[:, :, :], h_new[:, :, :]), "pool", s)
                    elif kind == "qk_split":
                        hf = a[0]
                        wait(pool, "act", img, s)
                        wait(pool, "dve", img, ("k_proj", hf, 1))
                        wait(pool, "pe", img, ("scores", 4), 1)
                        finish(pool.tensor_tensor(k_lo[:, hf, 0:L], gk[:, hf, :],
                                                  k_hi[:, hf, 0:L].bitcast(F32), ALU.subtract), "pool", s)
                    elif kind == "table_scatter":
                        wait(pool, "dve", img, ("slots", 1))
                        settle(pool)
                        for c in range(NC):
                            for k in range(2):
                                pool.indirect_dma_start(
                                    slot_table, bass.IndirectOffsetOnAxis(ap=slot_of[0:CH[c], k, c:c + 1], axis=0),
                                    rows[0:CH[c], k, c, :], None).then_inc(ready["table_rows_out"], 16)
                        if isinstance(img.i, int) and img.i == B:
                            overfull.append(short_or_whole(pool))
                        pool.wait_ge(ready["table_rows_out"], (img.i + 1) * (16 * 2 * NC))
                        pool.sem_inc(done["pool", "table_scatter"], 1)

            overfull = []
            pool.wait_ge(ready["table_out"], 17)
            images(pool, steps)
            attention_over(pool)
            for c in range(NC):
                wait(pool, "sp", image(LAST, B - 1), ("ln2_apply", c))
                wait(pool, "sp", image(LAST, B - 1), ("attn_out", c))
            pool.wait_ge(ready["zero_rows_out"], 32)
            experts(pool, expert_steps, overfull[0])

        @block.scalar
        def _(act):
            first_wait_credit(act, "act")
            link = Chain("act", act)
            loads = 0

            def load(dst, src, scattered=False):
                nonlocal loads
                act.dma_start(dst, src, allow_slow_non_contiguous=scattered).then_inc(ready["weights_in"], 16)
                loads += 1

            load(raw2[:, 0:DT * HD].rearrange("p (h r) -> p h r", h=DT), wg1.rearrange("(h p) r -> p h r", p=P))
            load(raw2[0:HD, D:2 * D], wg2)
            for n, w in enumerate((wq, wk, wg, wv)):
                load(raw13[:, n * 512:(n + 1) * 512].rearrange("p (h o) -> p h o", h=DT),
                     w.rearrange("(h p) o -> p h o", p=P))
            load(bias[:, :], bg2.rearrange("(h p) -> p h", p=P), scattered=True)
            load(wo_sb[:, :, :], wo.rearrange("(h p) o -> p h o", p=P))
            load(wr_sb[:, :, :], wr.rearrange("(h p) e -> p h e", p=P))
            for n in range(P // HD):
                load(gnw[n * HD:(n + 1) * HD, :], g_norm.rearrange("(v a) -> v a", a=1), scattered=True)
            assert loads == WEIGHT_LOADS
            for n in range(4):
                act.wait_ge(ready["we_turned"], n + 1)
                act.activation(we_hi[:, 2 * n:2 * n + 2, :], ps[n][:, :].rearrange("p (k o) -> p k o", k=2),
                               ACT.Copy).then_inc(ready["we_hi_made"], 1)
            act.wait_ge(ready["weights_in"], 16 * WEIGHT_LOADS)
            for n in range(4):
                act.activation(w5[:, n + 1, 0, :, :], raw13[:, n * 512:(n + 1) * 512].rearrange("p (h o) -> p h o", h=DT),
                               ACT.Copy).then_inc(ready["split_hi_made"], 1)
            act.wait_ge(ready["g1_turned"], 1)
            act.activation(raw2[0:HD, 2 * D:3 * D], ps[4][0:HD, 0:D], ACT.Copy).then_inc(ready["g1_copied"], 1)
            act.wait_ge(ready["g1_turned"], 2)
            act.activation(w5[:, 0, 0, :, :], ps[5][:, :].rearrange("p (h o) -> p h o", h=DT),
                           ACT.Copy).then_inc(ready["split_hi_made"], 1)

            def rsqrt(s, img, m, c, who):
                r = CH[c]
                wait(act, "dve", img, (who, c))
                wait(act, "dve", img, ("ln1_apply" if m == 0 else "ln2_apply", c), 1)
                link(act.activation(y0[0:r, m, c:c + 1], ve[0:r, m, c:c + 1], ACT.Ln))
                finish(act.activation(y0[0:r, m, c:c + 1], y0[0:r, m, c:c + 1], ACT.Exp, scale=-0.5), "act", s)

            ahead = expert(WHOLE, WHOLE.ahead, None)

            def expert_step(ex, s):
                kind, a = s[0], s[1:]
                if kind == "w13_split":
                    f = a[0]
                    wait(act, "sp", ex, ("load_w13", f // HALF))
                    if ex.i is None:
                        wait(act, "pe", image(BODY, B - 2), ("embed", 3))
                    else:
                        wait(act, "pe", ex, ("up", f, 1))
                    raw = raw13_half[f // HALF].rearrange("p (w k f) -> p w k f", w=2, k=DT)
                    cols = slice(f % HALF * P, (f % HALF + 1) * P)
                    for w in range(2):
                        ins = act.activation(w13[:, f, w, 0, :, :], raw[:, w, :, cols], ACT.Copy)
                    finish(ins, "act", s)
                elif kind == "w2_split":
                    f = a[0]
                    wait(act, "sp", ex, ("load_w2", f // HALF))
                    wait(act, "pe", ex, ("down", len(ex.cut.tiles) - 1), 1)
                    finish(act.activation(w2s[:, f, 0, :], raw2_half[f // HALF][:, f % HALF * D:(f % HALF + 1) * D], ACT.Copy), "act", s)
                elif kind == "xe_turn":
                    n = a[0]
                    o, r = ex.cut.tiles[n]
                    wait(act, "pe", ex, s)
                    if ex.i is not None:
                        wait(act, "pe", ex, ("up", FT - 1, 1))
                    finish(act.activation(xe_hi[:, :, o:o + r], ps[BANK[s]][:, 0:DT * r].rearrange("p (h t) -> p h t", h=DT),
                                          ACT.Copy), "act", s)
                elif kind == "up":
                    f, h = a
                    at, width = ex.cut.halves[h]
                    cols = slice(at, at + width)
                    wait(act, "pe", ex, s)
                    wait(act, "dve", ex, ("up", f - 1, h) if f else ("up", FT - 1, h), 0 if f else 1)
                    finish(act.activation(gate_flat[:, cols], ps[2 * h][:, 0:width], ACT.Silu), "act", s)
                elif kind == "h_split":
                    f, h = a
                    at, width = ex.cut.halves[h]
                    cols = slice(at, at + width)
                    wait(act, "dve", ex, ("up", f, h))
                    wait(act, "pe", ex, ("down", ex.cut.last[h]), 1)
                    finish(act.activation(h_hi[:, f, cols], dec_flat[:, cols], ACT.Copy),
                           "act", s)

            def expert_steps(ex):
                if ex.i is None:
                    act.preload_act_table_set("silu_and_others")
                for s in ex.steps:
                    if "act" in PARTS[s[0]]:
                        expert_step(ex, s)

            def steps(img):
                act.preload_act_table_set("natural_log_exp_and_others")
                for s in img.steps:
                    kind, a = s[0], s[1:]
                    if kind in NEXT_EXPERT:
                        expert_step(ahead, s)
                        continue
                    if kind == "x_turn":
                        c, q = a
                        wait(act, "pe", img, s)
                        wait(act, "pe", img, ("embed", c - 2 if c >= 2 else c + 2), 0 if c >= 2 else 1)
                        finish(act.activation(xt_hi[:, c % 2, 4 * q:4 * q + 4, :],
                                              ps[img.banks(s)[0]][:, :].rearrange("p (k t) -> p k t", k=4), ACT.Copy), "act", s)
                    elif kind == "embed":
                        c = a[0]
                        wait(act, "pe", img, s)
                        if img.i is not None:
                            wait(act, "pool", img, ("hold_residual",), 1)
                        finish(act.activation(h_new[:, c, :], ps[BANK[s]][:, 0:D], ACT.Copy), "act", s)
                    elif kind == "ln1_rsqrt":
                        rsqrt(s, img, 0, a[0], "ln1_stats")
                    elif kind == "ln2_rsqrt":
                        rsqrt(s, img, 1, a[0], "ln2_stats")
                    elif kind == "xn_turn":
                        c = a[0]
                        r = CH[c]
                        wait(act, "pe", img, s)
                        if img.i is not None:
                            wait(act, "pe", img, ("gate_proj", 1, 1))
                            wait(act, "pe", img, ("k_proj", 1, 1))
                        finish(act.activation(xn_hi[:, :, ST[c]:ST[c] + r],
                                              ps[BANK[s]][:, 0:DT * r].rearrange("p (h t) -> p h t", h=DT),
                                              ACT.Copy), "act", s)
                    elif kind == "decay_proj":
                        hf, n = a
                        wait(act, "pe", img, s)
                        wait(act, "pe", img, ("mix", 4))
                        wait(act, "dve", img, ("qk_split", 1))
                        wait(act, "act", img, ("qk_split", 1))
                        finish(act.activation(zq[:, hf, n * NW:(n + 1) * NW], ps[BANK[s]][:, 0:NW], ACT.Identity,
                                              bias=bias[:, hf:hf + 1]), "act", s)
                    elif kind == "decay_log":
                        hf = a[0]
                        wait(act, "dve", img, ("decay_abs", hf))
                        link(act.activation(gk[:, hf, :], gk[:, hf, :], ACT.Exp))
                        finish(act.activation(gk[:, hf, :], gk[:, hf, :], ACT.Ln, bias=ones[:, 0:1]), "act", s)
                    elif kind == "decay_exp":
                        hf = a[0]
                        wait(act, "dve", img, ("decay_sum", hf))
                        wait(act, "dve", img, ("state", 3))
                        act.activation(dec[:, hf, :], gk[:, hf, :], ACT.Exp, scale=1.0 / GLN)
                        finish(act.activation(gk[:, hf, :], gk[:, hf, :], ACT.Exp, scale=-1.0 / GLN), "act", s)
                    elif kind == "v_proj":
                        c = a[0]
                        r = CH[c]
                        wait(act, "pe", img, s)
                        wait(act, "pe", img, ("mix", c))
                        finish(act.activation(vp[0:r, c, :, 0:3:2, :],
                                              ps[BANK[s]][0:r, 0:D].rearrange("p (n e v) -> p n e v", e=2, v=HD),
                                              ACT.Copy), "act", s)
                    elif kind == "gate_proj":
                        hf, n = a
                        wait(act, "pe", img, s)
                        wait(act, "dve", img, ("mix", 4), 1)
                        finish(act.activation(gate[:, hf, n * NW:(n + 1) * NW], ps[BANK[s]][:, 0:NW], ACT.Silu), "act", s)
                        if a == (1, 1):
                            act.preload_act_table_set("natural_log_exp_and_others")
                    elif kind == "qk_split":
                        hf = a[0]
                        wait(act, "dve", img, ("q_proj", hf, 1))
                        wait(act, "dve", img, ("k_proj", hf, 1))
                        wait(act, "pe", img, ("scores", 4), 1)
                        for e in range(2):
                            act.activation(q_hi[:, hf, e, 0:L], zq[:, hf, :], ACT.Copy, scale=evenodd[:, e:e + 1])
                        finish(act.activation(k_hi[:, hf, 0:L], gk[:, hf, :], ACT.Copy), "act", s)
                    elif kind == "exact":
                        def exact_act(before):
                            base = before * EXACT_ACT
                            act.wait_ge(exact["dve"], before * EXACT_DVE + 17)
                            act.activation(ex_o, ex_o, ACT.Exp).then_inc(exact["act"], 1)
                            act.wait_ge(exact["act"], base + 1)
                            act.activation(ex_o, ex_o, ACT.Ln, bias=ones[:, 0:1]).then_inc(exact["act"], 1)
                            act.wait_ge(exact["dve"], before * EXACT_DVE + 18)
                            act.activation(ex_a, ex_a, ACT.Exp, scale=1.0 / GLN).then_inc(exact["act"], 1)

                        exact_path(act, img, exact_act)
                    elif kind == "k_turn":
                        c = a[0]
                        wait(act, "pe", img, s)
                        prev = ("state", c - 2) if c >= 2 else ("state", c + 2)
                        if c == 0:
                            act.wait_ge(ready["zero_rows_out"], 32)
                        wait(act, "pe", img, prev, 0 if c >= 2 else 1)
                        finish(act.activation(kt[:, c % 2, :], ps[BANK[s]][:, 0:D], ACT.Copy), "act", s)
                    elif kind == "mix":
                        c = a[0]
                        w = DT * CH[c]
                        wait(act, "pe", img, s)
                        wait(act, "pe", img, ("head_norm", c - 2) if c >= 2 else ("head_norm", 4), 0 if c >= 2 else 1)
                        finish(act.activation(sq[:, c % 2, 0:w], ps[4][:, 0:w], ACT.Square), "act", s)
                    elif kind == "head_norm":
                        c = a[0]
                        w = DT * CH[c]
                        wait(act, "pe", img, s)
                        wait(act, "dve", img, ("head_norm", c - 1) if c else ("head_norm", 4), 0 if c else 1)
                        link(act.activation(rs[:, 0:w], ps[BANK[s]][:, 0:w], ACT.Ln, bias=eps[:, 0:1], scale=1.0 / HD))
                        finish(act.activation(rs[:, 0:w], rs[:, 0:w], ACT.Exp, scale=-0.5), "act", s)
                    elif kind == "xn2_turn":
                        c = a[0]
                        r = CH[c]
                        wait(act, "pe", img, s)
                        wait(act, "pe", img, ("router", c - 2) if c >= 2 else ("router", 4), 0 if c >= 2 else 1)
                        finish(act.activation(x2t[:, c % 2, :, 0:r],
                                              ps[BANK[s]][:, 0:DT * r].rearrange("p (h t) -> p h t", h=DT),
                                              ACT.Copy), "act", s)
                    elif kind == "gate_exp":
                        wait(act, "dve", img, ("top2", 1))
                        finish(act.activation(tops[:, 2, :], tops[:, 2, :], ACT.Exp), "act", s)

            act.wait_ge(ready["consts_made"], CONSTS)
            act.wait_ge(ready["table_out"], 1)
            act.dma_start(slot_table.rearrange("(p j) t -> p j t", p=P), tinit[:, :, :]).then_inc(ready["table_out"], 16)
            for dst in (xn_rows, out_rows):
                act.dma_start(dst[T:T + SPARE, :].rearrange("(n p) d -> p n d", p=P),
                              kt[:, 0:1, :].to_broadcast([P, SPARE // P, D])).then_inc(ready["zero_rows_out"], 16)
            images(act, steps, link, ACT_CHAIN)
            attention_over(act)
            experts(act, expert_steps, short_or_whole(act))

        @block.vector
        def _(dve):
            first_wait_credit(dve, "dve")
            link = Chain("dve", dve)
            dve.memset(floor[:, :], FLOOR * GLN).then_inc(ready["exact_none"], 1)
            dve.memset(exact_f[:, :], 0.0).then_inc(ready["exact_none"], 1)
            dve.wait_ge(ready["exact_none"], 2)
            dve.wait_ge(ready["embed_weights_in"], 32)
            for hf in range(DT):
                dve.tensor_tensor(
                    prod[:, hf, :].rearrange("p (i d) -> p i d", d=DP),
                    xn[:, hf, :].rearrange("p (i a) -> p i a", a=1).to_broadcast([P, D, DP]),
                    tokw[:, hf:hf + 1, :].to_broadcast([P, D, DP]), ALU.mult).then_inc(ready["product_made"], 1)
            dve.wait_ge(ready["consts_made"], CONSTS)
            dve.tensor_reduce(evenodd[:, 0:1], blocks[:, 0:8:2, 0:1], AX.XY, ALU.add).then_inc(ready["product_made"], 1)
            dve.tensor_reduce(evenodd[:, 1:2], blocks[:, 1:8:2, 0:1], AX.XY, ALU.add).then_inc(ready["product_made"], 1)
            link(dve.tensor_scalar(tinit_i[:, :], tinit_i[:, :], SPARE - 1, None, ALU.bitwise_and))
            link(dve.tensor_copy(tinit[:, :, 0], tinit_i[:, :]))
            link(dve.tensor_scalar(tinit[:, :, 0], tinit[:, :, 0], float(T), None, ALU.add))
            dve.tensor_copy(tinit[:, :, 0].bitcast(I32), tinit[:, :, 0]).then_inc(ready["table_out"], 1)
            for n in range(4):
                dve.wait_ge(ready["we_hi_made"], n + 1)
                dve.tensor_tensor(we_lo[:, 2 * n:2 * n + 2, :], ps[n][:, :].rearrange("p (k o) -> p k o", k=2),
                                  we_hi[:, 2 * n:2 * n + 2, :].bitcast(F32), ALU.subtract).then_inc(ready["we_lo_made"], 1)
            for n in range(4):
                dve.wait_ge(ready["split_hi_made"], n + 1)
                dve.tensor_tensor(w5[:, n + 1, 1, :, :], raw13[:, n * 512:(n + 1) * 512].rearrange("p (h o) -> p h o", h=DT),
                                  w5[:, n + 1, 0, :, :].bitcast(F32), ALU.subtract).then_inc(ready["split_lo_made"], 1)
            dve.wait_ge(ready["split_hi_made"], 5)
            dve.tensor_tensor(w5[:, 0, 1, :, :], ps[5][:, :].rearrange("p (h o) -> p h o", h=DT),
                              w5[:, 0, 0, :, :].bitcast(F32), ALU.subtract).then_inc(ready["split_lo_made"], 1)

            def stats(s, src, m, c):
                r = CH[c]
                link(dve.bn_stats(bn[0:r, m, :], src[0:r, c, :]))
                settle(dve)
                link(dve.bn_aggr(mv[0:r, m, c, :], bn[0:r, m, :]))
                finish(dve.tensor_scalar(ve[0:r, m, c:c + 1], mv[0:r, m, c, 1:2], EPS, None, ALU.add), "dve", s)

            def normalise(s, dst, src, m, c):
                r = CH[c]
                y, v, t = y0[0:r, m, c:c + 1], ve[0:r, m, c:c + 1], y1[0:r, m, :]
                link(dve.scalar_tensor_tensor(t[:, 0:1], y, y, v, ALU.mult, ALU.mult))
                link(dve.tensor_scalar(t[:, 1:2], t[:, 0:1], -0.5, 1.5, ALU.mult, ALU.add))
                link(dve.tensor_tensor(t[:, 2:3], y, t[:, 1:2], ALU.mult))
                finish(dve.tensor_scalar(dst[0:r, c, :], src[0:r, c, :], mv[0:r, m, c, 0:1], t[:, 2:3],
                                         ALU.subtract, ALU.mult), "dve", s)

            ahead = expert(WHOLE, WHOLE.ahead, None)

            def expert_step(ex, s):
                kind, a = s[0], s[1:]
                if kind == "xe_turn":
                    n = a[0]
                    o, r = ex.cut.tiles[n]
                    wait(dve, "act", ex, s)
                    finish(dve.tensor_tensor(xe_lo[:, :, o:o + r],
                                             ps[BANK[s]][:, 0:DT * r].rearrange("p (h t) -> p h t", h=DT),
                                             xe_hi[:, :, o:o + r].bitcast(F32), ALU.subtract), "dve", s)
                elif kind == "up":
                    f, h = a
                    wait(dve, "act", ex, s)
                    wait(dve, "dve", ex, ("h_split", f - 1, h) if f else ("h_split", FT - 1, h), 0 if f else 1)
                    at, width = ex.cut.halves[h]
                    cols = slice(at, at + width)
                    finish(dve.tensor_tensor(dec_flat[:, cols], ps[2 * h + 1][:, 0:width], gate_flat[:, cols], ALU.mult),
                           "dve", s)
                elif kind == "h_split":
                    f, h = a
                    wait(dve, "act", ex, s)
                    at, width = ex.cut.halves[h]
                    cols = slice(at, at + width)
                    finish(dve.tensor_tensor(h_lo[:, f, cols], dec_flat[:, cols], h_hi[:, f, cols].bitcast(F32),
                                             ALU.subtract), "dve", s)
                elif kind == "down":
                    n = a[0]
                    r = ex.cut.tiles[n][1]
                    wait(dve, "pe", ex, s)
                    wait(dve, "sp", ex, ("load_scatter_index",))
                    wait(dve, "pool", ex, ("scattered",), 1)
                    finish(dve.tensor_scalar(ye[0:r, n, :], ps[BANK[s]][0:r, 0:D], s_index[0:r, n, 1:2], None,
                                             ALU.mult), "dve", s)

            def expert_steps(ex):
                for s in ex.steps:
                    if "dve" in PARTS[s[0]]:
                        expert_step(ex, s)

            def steps(img):
                for s in img.steps:
                    kind, a = s[0], s[1:]
                    if kind in NEXT_EXPERT:
                        expert_step(ahead, s)
                        continue
                    if kind == "x_turn":
                        c, q = a
                        wait(dve, "act", img, s)
                        finish(dve.tensor_tensor(xt_lo[:, c % 2, 4 * q:4 * q + 4, :],
                                                 ps[img.banks(s)[0]][:, :].rearrange("p (k t) -> p k t", k=4),
                                                 xt_hi[:, c % 2, 4 * q:4 * q + 4, :].bitcast(F32), ALU.subtract), "dve", s)
                    elif kind == "ln1_stats":
                        c = a[0]
                        if c < NC - 1:
                            wait(dve, "act", img, ("embed", c))
                        else:
                            wait(dve, "sp", img, ("load_txt",))
                        stats(s, h_new, 0, c)
                    elif kind == "ln1_apply":
                        c = a[0]
                        wait(dve, "act", img, ("ln1_rsqrt", c))
                        wait(dve, "pe", img, ("xn_turn", c), 1)
                        normalise(s, xn, h_new, 0, c)
                    elif kind == "ln2_stats":
                        wait(dve, "dve", img, ("attn_out", a[0]))
                        stats(s, h_res, 1, a[0])
                    elif kind == "ln2_apply":
                        c = a[0]
                        wait(dve, "act", img, ("ln2_rsqrt", c))
                        wait(dve, "pe", img, ("xn2_turn", c), 1)
                        wait(dve, "sp", img, s, 1)
                        normalise(s, xn2, h_res, 1, c)
                    elif kind == "xn_turn":
                        c = a[0]
                        r = CH[c]
                        wait(dve, "act", img, s)
                        finish(dve.tensor_tensor(xn_lo[:, :, ST[c]:ST[c] + r],
                                                 ps[BANK[s]][:, 0:DT * r].rearrange("p (h t) -> p h t", h=DT),
                                                 xn_hi[:, :, ST[c]:ST[c] + r].bitcast(F32), ALU.subtract), "dve", s)
                    elif kind == "decay_abs":
                        hf = a[0]
                        wait(dve, "act", img, ("decay_proj", hf, 1))
                        wait(dve, "pe", img, ("k_turn", 3))
                        wait(dve, "act", img, ("qk_split", 1))
                        wait(dve, "pool", img, ("qk_split", 1))
                        finish(dve.scalar_tensor_tensor(gk[:, hf, :], zq[:, hf, :], -1.0, zq[:, hf, :],
                                                        ALU.mult, ALU.min), "dve", s)
                    elif kind == "decay_sum":
                        hf = a[0]
                        wait(dve, "act", img, ("decay_log", hf))
                        link(dve.scalar_tensor_tensor(zq[:, hf, :], zq[:, hf, :], 0.0, gk[:, hf, :],
                                                      ALU.min, ALU.subtract))
                        for c in range(NC):
                            at_c = slice(ST[c], ST[c] + CH[c])
                            ins = dve.tensor_tensor_scan(gk[:, hf, at_c], zq[:, hf, at_c],
                                                         floor[:, 0:1].to_broadcast([P, CH[c]]), 0.0, ALU.add, ALU.max)
                        finish(ins, "dve", s)
                    elif kind == "range":
                        wait(dve, "act", img, ("decay_exp", 1))
                        dve.tensor_reduce(lowest[:, 0:1], dec[:, :, P - 1:S:P], AX.XY, ALU.min)
                        link(dve.tensor_reduce(lowest[:, 1:2], dec[:, :, L - 1:L], AX.XY, ALU.min))
                        finish(dve.tensor_scalar(lowest[:, :], lowest[:, :], LEAST, None, ALU.is_lt), "dve", s)
                    elif kind == "range_sum":
                        wait(dve, "pe", img, s)
                        link(dve.tensor_reduce(exact_f[:, 0:1], ps[BANK[s]][0:1, 0:2], AX.X, ALU.add))
                        link(dve.tensor_scalar(exact_f[:, 0:1], exact_f[:, 0:1], 0.0, None, ALU.is_gt))
                        link(dve.tensor_tensor(exact_f[:, 1:2], exact_f[:, 1:2], exact_f[:, 0:1], ALU.add))
                        finish(dve.tensor_tensor(exact_i[:, :], exact_f[:, 0:1], exact_f[:, 1:2], ALU.mult), "dve", s)
                    elif kind == "exact":
                        def exact_dve(before):
                            base = before * EXACT_DVE
                            pe_base = before * EXACT_PE
                            n_done = [0]

                            def linked(ins, at=None):
                                if at is None:
                                    n_done[0] += 1
                                    at = base + n_done[0]
                                ins.then_inc(exact["dve"], 1)
                                dve.wait_ge(exact["dve"], at)

                            wait(dve, "pe", img, ("mix", 4), 1)
                            wait(dve, "dve", img, ("scores", 4), 1)
                            wait(dve, "pe", img, ("xn2_turn", 4), 1)
                            for c in range(NC):
                                wait(dve, "sp", img, ("ln2_apply", c), 1)
                            wait(dve, "act", img, ("qk_split", 1))
                            wait(dve, "pool", img, ("qk_split", 1))
                            wait(dve, "dve", img, ("qk_split", 1))
                            wait(dve, "pool", img, ("hold_residual",), 1)
                            for i, (hf, n, w, dst) in enumerate(exact_products()):
                                dve.wait_ge(exact["pe"], pe_base + i + 1)
                                cols = slice(hf * L + n * NW, hf * L + (n + 1) * NW)
                                dst = {"z": ex_a, "q": ex_q, "k": ex_k, "v": ex_v}[dst][:, cols]
                                if w == 0:
                                    linked(dve.tensor_scalar(dst, ps[i % 4][:, 0:NW], bias[:, hf:hf + 1], None, ALU.add))
                                else:
                                    linked(dve.tensor_scalar(dst, ps[i % 4][:, 0:NW], QSCALE if w == 1 else 1.0, None,
                                                             ALU.mult))
                            linked(dve.scalar_tensor_tensor(ex_o, ex_a, -1.0, ex_a, ALU.mult, ALU.min))
                            dve.wait_ge(exact["act"], before * EXACT_ACT + 2)
                            linked(dve.scalar_tensor_tensor(ex_a, ex_a, 0.0, ex_o, ALU.min, ALU.subtract))
                            dve.wait_ge(exact["act"], before * EXACT_ACT + 3)
                            linked(dve.memset(ex_o, 0.0))
                            linked(dve.memset(hot, 0.0))
                            linked(dve.memset(hot[:, HD - 1:HD], 1.0))
                            linked(dve.tensor_reduce(onehot, ident[:, :].rearrange("p (n v) -> p v n", v=HD), AX.X, ALU.add))
                            settle(dve)
                            with dve.Fori(0, HD) as v:
                                at_v, pe_v = base + n_done[0] + v * 14, pe_base + 16 + v * 4
                                linked(dve.tensor_scalar(sel_in, blocks[:, :, :], onehot[:, bass.ds(v, 1)], None, ALU.mult),
                                       at_v + 1)
                                settle(dve)
                                linked(dve.tensor_tensor(sel_out, blocks[:, :, :],
                                                         hot[:, bass.ds(HD - 1 - v, HD)].rearrange("p (a v) -> p a v", a=1)
                                                         .to_broadcast([P, P // HD, HD]), ALU.mult), at_v + 2)
                                for hf in range(DT):
                                    at = at_v + 2 + 6 * hf
                                    dve.wait_ge(exact["pe"], pe_v + 2 * hf + 1)
                                    for n in range(2):
                                        cols = slice(n * NW, (n + 1) * NW)
                                        linked(dve.tensor_tensor(ex_u[:, cols], ps[n][:, 0:NW],
                                                                 ex_k[:, hf * L + n * NW:hf * L + (n + 1) * NW], ALU.mult),
                                               at + n + 1)
                                    linked(dve.tensor_tensor_scan(ex_s, ex_a[:, hf * L:(hf + 1) * L], ex_u, 0.0,
                                                                  ALU.mult, ALU.add), at + 3)
                                    linked(dve.tensor_tensor(ex_w, ex_s, ex_q[:, hf * L:(hf + 1) * L], ALU.mult), at + 4)
                                    dve.wait_ge(exact["pe"], pe_v + 2 * hf + 2)
                                    for n in range(2):
                                        dst = ex_o[:, hf * L + n * NW:hf * L + (n + 1) * NW]
                                        linked(dve.tensor_tensor(dst, dst, ps[2 + n][:, 0:NW], ALU.add), at + 5 + n)
                                settle(dve)
                            n_done[0] += HD * 14
                            linked(dve.memset(k_hi[:, :, 0:L].bitcast(F32), 0.0))
                            linked(dve.memset(k_lo[:, :, 0:L].bitcast(F32), 0.0))
                            linked(dve.memset(gk[:, :, :], 0.0))
                            linked(dve.memset(dec[:, :, :], 1.0))
                            for hf in range(DT):
                                linked(dve.tensor_copy(state0[:, hf, :], ident[:, :]))
                            settle(dve)
                            assert n_done[0] == EXACT_DVE, n_done[0]

                        exact_path(dve, img, exact_dve)
                        dve.sem_inc(done["dve", "exact"], 1)
                    elif kind == "q_proj":
                        hf, n = a
                        w = slice(n * NW, (n + 1) * NW)
                        wait(dve, "pe", img, s)
                        wait(dve, "act", img, ("decay_exp", hf), 1)
                        finish(dve.scalar_tensor_tensor(zq[:, hf, w], ps[BANK[s]][:, 0:NW], QSCALE, dec[:, hf, w],
                                                        ALU.mult, ALU.mult), "dve", s)
                    elif kind == "k_proj":
                        hf, n = a
                        w = slice(n * NW, (n + 1) * NW)
                        wait(dve, "pe", img, s)
                        wait(dve, "act", img, ("decay_exp", hf), 1)
                        finish(dve.tensor_tensor(gk[:, hf, w], ps[BANK[s]][:, 0:NW], gk[:, hf, w], ALU.mult), "dve", s)
                    elif kind == "qk_split":
                        hf = a[0]
                        wait(dve, "act", img, s)
                        wait(dve, "dve", img, ("q_proj", hf, 1))
                        for e in range(2):
                            ins = dve.scalar_tensor_tensor(q_lo[:, hf, e, 0:L], zq[:, hf, :], evenodd[:, e:e + 1],
                                                           q_hi[:, hf, e, 0:L].bitcast(F32), ALU.mult, ALU.subtract)
                        finish(ins, "dve", s)
                    elif kind == "scores":
                        c = a[0]
                        r = CH[c]
                        wait(dve, "pe", img, s)
                        wait(dve, "pe", img, ("mix", c - 2) if c >= 2 else ("mix", 4), 0 if c >= 2 else 1)
                        for j in range(4):
                            ins = dve.tensor_tensor(att[0:r, c % 2, j, :, 0:r],
                                                    ps[j][0:r, 0:4 * r].rearrange("p (n t) -> p n t", n=4),
                                                    upper[0:r, 0:r].rearrange("p (a t) -> p a t", a=1)
                                                    .to_broadcast([r, 4, r]), ALU.mult)
                        finish(ins, "dve", s)
                    elif kind == "state":
                        c = a[0]
                        wait(dve, "pe", img, s)
                        if c >= 1:
                            wait(dve, "pe", img, ("mix", c - 1))
                        else:
                            wait(dve, "pe", img, ("mix", 4), 1)
                        wait(dve, "pool", img, ("hold_residual",), 1)
                        end = ST[c] + P - 1
                        for hf in range(DT):
                            old = state[:, c % 2, hf, :] if c else state0[:, hf, :]
                            link(dve.scalar_tensor_tensor(stmp[:, hf, :], ps[BANK[s]][:, hf * P:(hf + 1) * P],
                                                          dec[:, hf, end:end + 1],
                                                          blocks[:, :, :].rearrange("p n v -> p (n v)"),
                                                          ALU.mult, ALU.mult))
                            ins = dve.scalar_tensor_tensor(state[:, (c + 1) % 2, hf, :], old, dec[:, hf, end:end + 1],
                                                           stmp[:, hf, :], ALU.mult, ALU.add)
                        finish(ins, "dve", s)
                    elif kind == "mix":
                        c = a[0]
                        r = CH[c]
                        wait(dve, "act", img, s)
                        wait(dve, "act", img, ("gate_proj", 1, 1))
                        wait(dve, "pe", img, ("attn_out", c - 2) if c >= 2 else ("attn_out", 4), 0 if c >= 2 else 1)
                        finish(dve.scalar_tensor_tensor(og[:, c % 2, :, 0:r],
                                                        ps[4][:, 0:DT * r].rearrange("p (h t) -> p h t", h=DT),
                                                        gnw[:, 0:1], gate[:, :, ST[c]:ST[c] + r],
                                                        ALU.mult, ALU.mult), "dve", s)
                    elif kind == "head_norm":
                        c = a[0]
                        r = CH[c]
                        wait(dve, "act", img, s)
                        wait(dve, "dve", img, ("mix", c))
                        finish(dve.tensor_tensor(og[:, c % 2, :, 0:r], og[:, c % 2, :, 0:r],
                                                 rs[:, 0:DT * r].rearrange("p (h t) -> p h t", h=DT), ALU.mult), "dve", s)
                    elif kind == "attn_out":
                        c = a[0]
                        r = CH[c]
                        wait(dve, "pe", img, s)
                        wait(dve, "pool", img, ("hold_residual",), 1)
                        finish(dve.tensor_tensor(h_res[0:r, c, :], ps[BANK[s]][0:r, 0:D], h_res[0:r, c, :], ALU.add),
                               "dve", s)
                    elif kind == "router":
                        c = a[0]
                        r = CH[c]
                        wait(dve, "pe", img, s)
                        finish(dve.tensor_scalar(lg[0:r, c, :], ps[BANK[s]][0:r, 0:E], CLAMP, -CLAMP, ALU.min, ALU.max),
                               "dve", s)
                    elif kind == "top2":
                        k = a[0]

                        def over_experts(v):
                            return v.rearrange("p (c a) -> p c a", a=1).to_broadcast([P, NC, E])

                        if k == 0:
                            wait(dve, "dve", img, ("router", 4), 1)
                            wait(dve, "dve", img, ("slots", 1), 1)
                            wait(dve, "pe", img, ("rank",), 1)
                            wait(dve, "pool", img, ("table_scatter",), 1)
                            link(dve.tensor_scalar(token_no[:, :], token_no[:, :], float(L), None, ALU.add))
                        else:
                            wait(dve, "dve", img, ("top2", 0))
                        fall = falling[:, :].rearrange("p (a e) -> p a e", a=1).to_broadcast([P, NC, E])
                        src = work[:, 1] if k else lg[:, :, :]
                        link(dve.tensor_reduce(tops[:, k, :], src, AX.X, ALU.max))
                        link(dve.tensor_tensor(work[:, 0], src, over_experts(tops[:, k, :]), ALU.is_equal))
                        link(dve.tensor_tensor(work[:, 0], work[:, 0], fall, ALU.mult))
                        link(dve.tensor_reduce(tops[:, 3, :], work[:, 0], AX.X, ALU.max))
                        link(dve.tensor_tensor(pick[:, k], work[:, 0], over_experts(tops[:, 3, :]), ALU.is_equal))
                        if k == 0:
                            ins = dve.scalar_tensor_tensor(work[:, 1], pick[:, 0], -3.0e38, lg[:, :, :],
                                                           ALU.mult, ALU.add)
                        else:
                            link(dve.tensor_tensor(tops[:, 2, :], tops[:, 1, :], tops[:, 0, :], ALU.subtract))
                            link(dve.tensor_tensor(work[:, 0], pick[:, 0], pick[:, 1], ALU.add))
                            link(dve.tensor_tensor(work[:, 0], work[:, 0], over_experts(valid[:, 0, :]), ALU.mult))
                            link(dve.tensor_copy(cum[:, 0, :], cum[:, NC, :]))
                            for c in range(NC):
                                ins = dve.tensor_tensor(cum[:, c + 1, :], cum[:, c, :], work[:, 0, c, :], ALU.add)
                                if c < NC - 1:
                                    link(ins)
                        finish(ins, "dve", s)
                    elif kind == "slots":
                        if a[0] == 0:
                            wait(dve, "act", img, ("gate_exp",))
                            w1k, w2k = tops[:, 0, :], tops[:, 1, :]
                            link(dve.tensor_scalar(w1k, tops[:, 2, :], 1.0, 1e-12, ALU.add, ALU.add))
                            link(dve.reciprocal(w1k, w1k))
                            link(dve.tensor_tensor(w2k, tops[:, 2, :], w1k, ALU.mult))
                            for k in range(2):
                                dve.tensor_copy(rows[:, k, :, 1], tops[:, k, :])
                                dve.tensor_scalar(rows[:, k, :, 0].bitcast(I32), token_no[:, :], 0.0, None, ALU.max)
                            wait(dve, "pe", img, ("rank",))
                            rank = ps[BANK["rank",]][:, 0:NC * E].rearrange("p (c e) -> p c e", c=NC)
                            link(dve.tensor_tensor(work[:, 1], rank, pick[:, 1], ALU.mult))
                            link(dve.tensor_reduce(posk[:, 0, 1, :], work[:, 1], AX.X, ALU.add))
                            finish(dve.tensor_tensor(work[:, 1], rank, pick[:, 0], ALU.mult), "dve", s)
                        else:
                            wait(dve, "dve", img, ("slots", 0))
                            link(dve.tensor_reduce(posk[:, 0, 0, :], work[:, 1], AX.X, ALU.add))
                            eno = expert_no[:, :].rearrange("p (a e) -> p a e", a=1).to_broadcast([P, NC, E])
                            for k in range(2):
                                link(dve.tensor_tensor(work[:, 1], pick[:, k], eno, ALU.mult))
                                link(dve.tensor_reduce(posk[:, 1, k, :], work[:, 1], AX.X, ALU.add))
                            past = dump[:, :, :]
                            link(dve.tensor_scalar(posk[:, 2], posk[:, 0], float(CAP), None, ALU.is_lt))
                            link(dve.scalar_tensor_tensor(posk[:, 1], posk[:, 1], float(CAP), posk[:, 0],
                                                          ALU.mult, ALU.add))
                            link(dve.tensor_tensor(posk[:, 1], posk[:, 1], past, ALU.subtract))
                            link(dve.tensor_tensor(posk[:, 2], posk[:, 2], valid[:, :, :], ALU.mult))
                            link(dve.tensor_tensor(posk[:, 1], posk[:, 1], posk[:, 2], ALU.mult))
                            link(dve.tensor_tensor(posk[:, 1], posk[:, 1], past, ALU.add))
                            link(dve.tensor_copy(valid[:, :, :], valid_rows[:, :, :]))
                            finish(dve.tensor_copy(slot_of[:, :, :], posk[:, 1]), "dve", s)

            dve.wait_ge(ready["pads_zeroed"], 1)
            images(dve, steps, link, DVE_CHAIN)
            wait(dve, "dve", image(ROUTE, B), ("slots", 1))
            dve.wait_ge(ready["counts_summed"], 1)
            dve.tensor_reduce(overfull_f[:, :], ps[4][0:1, 0:E], AX.X, ALU.max).then_inc(ready["most_found"], 1)
            dve.wait_ge(ready["most_found"], 1)
            dve.tensor_scalar(overfull_i[:, :], overfull_f[:, :], float(SHORT.slots), None,
                              ALU.is_gt).then_inc(ready["cut_known"], 1)
            attention_over(dve)
            experts(dve, expert_steps, short_or_whole(dve))

        @block.tensor
        def _(pe):
            first_wait_credit(pe, "pe")
            pe.wait_ge(ready["product_made"], 2)
            pe.wait_ge(ready["consts_made"], CONSTS)
            for n in range(4):
                for kk in range(2):
                    for hf in range(DT):
                        ins = pe.transpose(ps[n][:, (2 * kk + hf) * P:(2 * kk + hf + 1) * P],
                                           prod[:, hf, (2 * n + kk) * P:(2 * n + kk + 1) * P], ident[:, :])
                ins.then_inc(ready["we_turned"], 1)
            pe.wait_ge(ready["weights_in"], 16 * WEIGHT_LOADS)
            for hf in range(DT):
                ins = pe.matmul(ps[4][0:HD, hf * P:(hf + 1) * P], raw2[:, hf * HD:(hf + 1) * HD], ident[:, :],
                                start=True, stop=True)
            ins.then_inc(ready["g1_turned"], 1)
            pe.wait_ge(ready["g1_copied"], 1)
            for hf in range(DT):
                ins = pe.matmul(ps[5][:, hf * D:(hf + 1) * D], raw2[0:HD, 2 * D + hf * P:2 * D + (hf + 1) * P],
                                raw2[0:HD, D:2 * D], start=True, stop=True)
            ins.then_inc(ready["g1_turned"], 1)
            def three(out_ap, pairs):
                n = 3 * len(pairs)
                i = 0
                for (a_hi, a_lo), (b_hi, b_lo) in pairs:
                    for lhs, rhs in ((a_hi, b_hi), (a_hi, b_lo), (a_lo, b_hi)):
                        ins = pe.matmul(out_ap, lhs, rhs, start=(i == 0), stop=(i == n - 1))
                        i += 1
                return ins

            ahead = expert(WHOLE, WHOLE.ahead, None)

            def expert_step(ex, s):
                kind, a = s[0], s[1:]
                bank_free(pe, ex, s)
                if kind == "xe_turn":
                    n = a[0]
                    r = ex.cut.tiles[n][1]
                    wait(pe, "pool", ex, ("gather", n))
                    for hf in range(DT):
                        ins = pe.transpose(ps[BANK[s]][:, hf * r:(hf + 1) * r], xe[0:r, n, hf * P:(hf + 1) * P],
                                           ident[0:r, 0:r])
                    finish(ins, "pe", s)
                elif kind == "up":
                    f, h = a
                    wait(pe, "pool", ex, ("w13_split", f), 1)
                    wait(pe, "dve", ex, ("xe_turn", ex.cut.last[h]), 1)
                    at, width = ex.cut.halves[h]
                    cols = slice(at, at + width)
                    for w in range(2):
                        ins = three(ps[2 * h + w][:, 0:width], [((w13[:, f, w, 0, k, :], w13[:, f, w, 1, k, :]),
                                                              (xe_hi[:, k, cols], xe_lo[:, k, cols])) for k in range(DT)])
                    finish(ins, "pe", s)
                elif kind == "down":
                    n = a[0]
                    o, r = ex.cut.tiles[n]
                    h = ex.cut.half_of[n]
                    wait(pe, "pool", ex, ("w2_split", FT - 1))
                    for f in range(FT):
                        if f == FT - 1:
                            wait(pe, "dve", ex, ("h_split", f, h))
                        elif f == 0:
                            wait(pe, "dve", ex, ("h_split", FT - 2, h))
                        for i, (hh, ww) in enumerate(((h_hi, 0), (h_hi, 1), (h_lo, 0))):
                            ins = pe.matmul(ps[BANK[s]][0:r, 0:D], hh[:, f, o:o + r], w2s[:, f, ww, :],
                                            start=(f == 0 and i == 0), stop=(f == FT - 1 and i == 2))
                    finish(ins, "pe", s)

            def expert_steps(ex):
                for s in ex.steps:
                    if "pe" in PARTS[s[0]]:
                        expert_step(ex, s)

            def steps(img):
                for s in img.steps:
                    kind, a = s[0], s[1:]
                    if kind in NEXT_EXPERT:
                        expert_step(ahead, s)
                        continue
                    if "pe" in PARTS[kind]:
                        bank_free(pe, img, s)
                    bank = ps[img.banks(s)[0]] if s in BANK else None
                    if kind == "x_turn":
                        c, q = a
                        wait(pe, "sp", img, ("load_x", c))
                        if img.i is None and c < 2:
                            pe.wait_ge(ready["we_lo_made"], img.banks(s)[0] + 1)
                        for j in range(4):
                            ins = pe.transpose(bank[:, j * P:(j + 1) * P],
                                               x_in[:, c % 2, (4 * q + j) * P:(4 * q + j + 1) * P], ident[:, :])
                        finish(ins, "pe", s)
                    elif kind == "embed":
                        c = a[0]
                        wait(pe, "dve", img, ("x_turn", c, 1))
                        if img.i is None:
                            pe.wait_ge(ready["we_lo_made"], 4)
                            pe.wait_ge(ready["split_lo_made"], 5)
                        r = c % 2
                        finish(three(bank[:, 0:D], [((xt_hi[:, r, k, :], xt_lo[:, r, k, :]), (we_hi[:, k, :], we_lo[:, k, :]))
                                                    for k in range(KT)]), "pe", s)
                    elif kind == "xn_turn":
                        c = a[0]
                        r = CH[c]
                        wait(pe, "dve", img, ("ln1_apply", c))
                        settle(pe)
                        for hf in range(DT):
                            ins = pe.transpose(bank[:, hf * r:(hf + 1) * r], xn[0:r, c, hf * P:(hf + 1) * P],
                                               ident[0:r, 0:r])
                        finish(ins, "pe", s)
                    elif kind in ("decay_proj", "q_proj", "k_proj", "gate_proj"):
                        hf, n = a
                        if kind == "decay_proj":
                            wait(pe, "dve", img, ("xn_turn", 3))
                        w = {"decay_proj": 0, "q_proj": 1, "k_proj": 2, "gate_proj": 3}[kind]
                        o, t = slice(hf * P, (hf + 1) * P), slice(n * NW, (n + 1) * NW)
                        finish(three(bank[:, 0:NW], [((w5[:, w, 0, k, o], w5[:, w, 1, k, o]),
                                                      (xn_hi[:, k, t], xn_lo[:, k, t])) for k in range(DT)]), "pe", s)
                    elif kind == "v_proj":
                        c = a[0]
                        t = slice(ST[c], ST[c] + P)
                        wait(pe, "dve", img, ("xn_turn", c))
                        finish(three(bank[:, 0:D], [((xn_hi[:, k, t], xn_lo[:, k, t]),
                                                     (w5[:, 4, 0, k, :], w5[:, 4, 1, k, :])) for k in range(DT)]), "pe", s)
                    elif kind == "range_sum":
                        wait(pe, "dve", img, ("range",))
                        finish(pe.matmul(bank[0:1, 0:2], ones[:, 0:1], lowest[:, :], start=True, stop=True), "pe", s)
                    elif kind == "exact":
                        bank_free(pe, img, s)

                        def exact_pe(before):
                            base, dve_base = before * EXACT_PE, before * EXACT_DVE
                            for i, (hf, n, w, _) in enumerate(exact_products()):
                                if i >= 4:
                                    pe.wait_ge(exact["dve"], dve_base + i - 3)
                                o, t = slice(hf * P, (hf + 1) * P), slice(n * NW, (n + 1) * NW)
                                three(ps[i % 4][:, 0:NW], [((w5[:, w, 0, k, o], w5[:, w, 1, k, o]),
                                                            (xn_hi[:, k, t], xn_lo[:, k, t])) for k in range(DT)]
                                      ).then_inc(exact["pe"], 1)
                            with pe.Fori(0, HD) as v:
                                at_v = dve_base + 22 + v * 14
                                for hf in range(DT):
                                    at = at_v + 2 + 6 * hf
                                    pe.wait_ge(exact["dve"], at)
                                    for n in range(2):
                                        ins = pe.matmul(ps[n][:, 0:NW], sel_in.rearrange("p n v -> p (n v)"),
                                                        ex_v[:, hf * L + n * NW:hf * L + (n + 1) * NW],
                                                        start=True, stop=True)
                                    ins.then_inc(exact["pe"], 1)
                                    pe.wait_ge(exact["dve"], at + 4)
                                    for n in range(2):
                                        ins = pe.matmul(ps[2 + n][:, 0:NW], sel_out.rearrange("p n v -> p (n v)"),
                                                        ex_w[:, n * NW:(n + 1) * NW], start=True, stop=True)
                                    ins.then_inc(exact["pe"], 1)

                        exact_path(pe, img, exact_pe)
                    elif kind == "scores":
                        c = a[0]
                        r = CH[c]
                        if c == 0:
                            wait(pe, "dve", img, ("exact",))
                            wait(pe, "dve", img, ("qk_split", 1))
                            wait(pe, "pool", img, ("qk_split", 1))
                        for hf in range(DT):
                            for n, (kk, qq) in enumerate(((k_hi, q_hi), (k_hi, q_lo), (k_lo, q_hi))):
                                for j in range(4):
                                    rows_j = slice(32 * j, 32 * j + 32)
                                    ins = pe.matmul(ps[j][:, hf * 2 * r:(hf + 1) * 2 * r].rearrange("p (e t) -> p e t", e=2),
                                                    kk[rows_j, hf, ST[c]:ST[c] + P], qq[rows_j, hf, :, ST[c]:ST[c] + r],
                                                    start=(n == 0), stop=(n == 2))
                        finish(ins, "pe", s)
                    elif kind == "k_turn":
                        c = a[0]
                        for hf in range(DT):
                            ins = pe.transpose(bank[:, hf * P:(hf + 1) * P], gk[:, hf, ST[c]:ST[c] + P], ident[:, :])
                        finish(ins, "pe", s)
                    elif kind == "state":
                        c = a[0]
                        wait(pe, "act", img, ("k_turn", c))
                        wait(pe, "act", img, ("v_proj", 4), 1)
                        for hf in range(DT):
                            ins = pe.matmul(bank[:, hf * P:(hf + 1) * P].rearrange("p (n e v) -> p n e v", n=4, e=2),
                                            kt[:, c % 2, hf * P:(hf + 1) * P],
                                            vp[:, c, 4 * hf:4 * hf + 4, 0:3:2, :], start=True, stop=True)
                        finish(ins, "pe", s)
                    elif kind == "mix":
                        c = a[0]
                        r = CH[c]
                        wait(pe, "dve", img, ("scores", c))
                        if c:
                            wait(pe, "dve", img, ("state", c - 1))
                        for hf in range(DT):
                            cols = slice(hf * r, (hf + 1) * r)
                            pe.matmul(bank[:, cols], state[:, c % 2, hf, :] if c else state0[:, hf, :],
                                      zq[:, hf, ST[c]:ST[c] + r], start=True, stop=False, skip_group_check=True)
                            for e in range(2):
                                for j in range(4):
                                    v48 = vp[0:r, c, 4 * hf + j, :, :].rearrange("p a v -> p (a v)")
                                    ins = pe.matmul(bank[32 * j:32 * j + 32, cols], v48[:, e * HD:e * HD + 2 * HD],
                                                    att[0:r, c % 2, j, 2 * hf + e, 0:r],
                                                    start=False, stop=(e == 1), skip_group_check=True)
                        finish(ins, "pe", s)
                    elif kind == "head_norm":
                        c = a[0]
                        w = DT * CH[c]
                        wait(pe, "act", img, ("mix", c))
                        finish(pe.matmul(bank[:, 0:w], blocks[:, :, :].rearrange("p n v -> p (n v)"), sq[:, c % 2, 0:w],
                                         start=True, stop=True), "pe", s)
                    elif kind == "attn_out":
                        c = a[0]
                        r = CH[c]
                        wait(pe, "dve", img, ("head_norm", c))
                        for hf in range(DT):
                            ins = pe.matmul(bank[0:r, 0:D], og[:, c % 2, hf, 0:r], wo_sb[:, hf, :],
                                            start=(hf == 0), stop=(hf == 1))
                        finish(ins, "pe", s)
                    elif kind == "xn2_turn":
                        c = a[0]
                        r = CH[c]
                        wait(pe, "dve", img, ("ln2_apply", c))
                        settle(pe)
                        for hf in range(DT):
                            ins = pe.transpose(bank[:, hf * r:(hf + 1) * r], xn2[0:r, c, hf * P:(hf + 1) * P],
                                               ident[0:r, 0:r])
                        finish(ins, "pe", s)
                    elif kind == "router":
                        c = a[0]
                        r = CH[c]
                        wait(pe, "act", img, ("xn2_turn", c))
                        for hf in range(DT):
                            ins = pe.matmul(bank[0:r, 0:E], x2t[:, c % 2, hf, 0:r], wr_sb[:, hf, :],
                                            start=(hf == 0), stop=(hf == 1))
                        finish(ins, "pe", s)
                    elif kind == "rank":
                        wait(pe, "dve", img, ("top2", 1))
                        for c in range(NC):
                            r = CH[c]
                            pe.matmul(bank[0:r, c * E:(c + 1) * E], strict[0:r, 0:r], work[0:r, 0, c, :],
                                      start=True, stop=False)
                            ins = pe.matmul(bank[0:r, c * E:(c + 1) * E], ones[:, 0:r], cum[:, c, :],
                                            start=False, stop=True)
                        finish(ins, "pe", s)

            images(pe, steps)
            wait(pe, "dve", image(LAST, B - 1), ("mix", 4))
            wait(pe, "dve", image(ROUTE, B), ("top2", 1))
            pe.matmul(ps[4][0:1, 0:E], ones[:, 0:1], cum[:, NC, :], start=True, stop=True).then_inc(
                ready["counts_summed"], 1)
            attention_over(pe)
            experts(pe, expert_steps, short_or_whole(pe))


LEAST, FLOOR = 1e-26, -70.0
EXACT_PE = 16 + 4 * HD
EXACT_ACT = 3
EXACT_DVE = 22 + 14 * HD + 6


def exact_products():
    return [(hf, n, w, name) for hf in range(DT) for n in range(2)
            for w, name in ((0, "z"), (1, "q"), (2, "k"), (4, "v"))]


WEIGHT_LOADS = 17
CONSTS = 21
ACT_CHAIN = 17
DVE_CHAIN = 100

_INS = ["x", "txt", "L0_tok_weight", "L0_tok_weighted_sum", "L0_attn_Wq", "L0_attn_Wk", "L0_attn_Wv", "L0_attn_Wg1",
        "L0_attn_Wg2", "L0_attn_bg2", "L0_attn_Wg", "L0_attn_g_norm_w", "L0_attn_Wo", "L0_ffn_Wr", "L0_ffn_W1",
        "L0_ffn_W3", "L0_ffn_W2"]


def build(nc, args, out):
    slot_table = nc.dram_tensor("slot_table", (TABLE, 2), F32).ap()
    xn_rows = nc.dram_tensor("xn_rows", (T + SPARE, D), F32).ap()
    fusion_kernel(nc, *args, out, slot_table, xn_rows)


def kernel(**inputs):
    import concourse.bacc as bacc
    from concourse.bass_utils import run_bass_kernel_spmd

    nc = bacc.Bacc("TRN2", target_bir_lowering=False, num_devices=1)
    arrays, args = {}, []
    for name in _INS:
        a = np.ascontiguousarray(inputs[name])
        arrays[f"in_{name}"] = a
        args.append(nc.dram_tensor(f"in_{name}", a.shape, mybir.dt.from_np(a.dtype), kind="ExternalInput").ap())
    out = nc.dram_tensor("out_rows", (T + SPARE, D), F32, kind="ExternalOutput").ap()
    build(nc, args, out)
    result = run_bass_kernel_spmd(nc, [arrays], core_ids=[0]).results[0]["out_rows"]
    return result[:T].reshape(B, L, D)
```
